# Optimizing a Trainium2 kernel written in Bass

```python
import numpy as np
import jax
import jax.numpy as jnp

def _softmax(x, axis=-1):
    return jax.nn.softmax(x, axis=axis)

def _gelu(x):
    return jax.nn.gelu(x, approximate=True)

def _silu(x):
    return jax.nn.silu(x)

def _sigmoid(x):
    return jax.nn.sigmoid(x)

def _layernorm(x, axis=-1, eps=1e-05):
    m = jnp.mean(x, axis=axis, keepdims=True)
    v = jnp.var(x, axis=axis, keepdims=True)
    return (x - m) / jnp.sqrt(v + eps)

def _scatter_add(tgt, idx, src, axis=0):
    return tgt.at[idx].add(src)

def _segment_sum(src, seg, n):
    return jax.ops.segment_sum(src, seg, n)
kernel_name = 'mk_xattn_ffn_d1_seqx_r8_f76f14'

def setup_inputs(seed: int=0):
    np.random.seed(seed)
    _w = jnp.asarray

    def _rec_inputs():
        import jax
        import jax.numpy as jnp
        _rk = jax.random.key(seed)
        x = -0.000125 + 0.9999 * jax.random.normal(jax.random.fold_in(_rk, 1), (4, 256, 128), jnp.float32)
        _lenS = 256 - jax.random.randint(jax.random.fold_in(_rk, 7), (4,), 0, max(1, 256 // 4) + 1, jnp.int32)
        _lenS2 = 256 - jax.random.randint(jax.random.fold_in(_rk, 8), (4,), 0, max(1, 256 // 4) + 1, jnp.int32)
        _ctx_2048P = jax.random.normal(jax.random.fold_in(_rk, 11), (4, 16, 256), jnp.float32)
        _ctx_2048c = jax.random.dirichlet(jax.random.fold_in(_rk, 511), 0.3 * jnp.ones((16,), jnp.float32), (4, 256))
        _ctx_2048t = jnp.einsum('bsk,bkd->bsd', _ctx_2048c, _ctx_2048P)
        _ctx_2048t = _ctx_2048t * jax.lax.rsqrt(jnp.mean(jnp.square(_ctx_2048t)) + 1e-12) * 0.953939
        ctx_2048 = -1.39393e-06 + 0.999914 * (_ctx_2048t + 0.3 * jax.random.normal(jax.random.fold_in(_rk, 611), (4, 256, 256), jnp.float32))
        return (x, ctx_2048)
    x, ctx_2048 = _rec_inputs()

    def _L0_xattn_setup():
        import jax, jax.numpy as jnp
        import numpy as np
        B, N, DIM = (8, 512, 128)
        M, CTX = (32, 256)
        HEADS, DH = (16, 64)
        INNER = HEADS * DH
        EPS = 1e-06

        def _split_heads(t):
            b, n, _ = t.shape
            return t.reshape(b, n, HEADS, DH).transpose(0, 2, 1, 3)
        key = jax.random.key(seed)
        ks = jax.random.split(key, 6)
        x = jax.random.normal(ks[0], (B, N, DIM), dtype=jnp.float32)
        context = jax.random.normal(ks[1], (B, M, CTX), dtype=jnp.float32)
        Wq = jax.random.normal(ks[2], (DIM, INNER), dtype=jnp.float32) / np.sqrt(DIM)
        Wkv = jax.random.normal(ks[3], (CTX, 2 * INNER), dtype=jnp.float32) / np.sqrt(CTX)
        null_kv = jax.random.normal(ks[4], (2, DH), dtype=jnp.float32) / np.sqrt(2.0)
        Wout = jax.random.normal(ks[5], (INNER, DIM), dtype=jnp.float32) / np.sqrt(INNER)
        ln_scale = jnp.ones((DIM,), dtype=jnp.float32)
        ln_bias = jnp.zeros((DIM,), dtype=jnp.float32)
        return {'x': x, 'context': context, 'Wq': Wq, 'Wkv': Wkv, 'null_kv': null_kv, 'Wout': Wout, 'ln_scale': ln_scale, 'ln_bias': ln_bias}
    _L0_xattn_all = _L0_xattn_setup()
    _L0_xattn_in = {k: v for k, v in _L0_xattn_all.items() if k in ('Wq', 'Wkv', 'null_kv', 'Wout', 'ln_scale', 'ln_bias')}
    del _L0_xattn_all

    def _L0_ffn_setup():
        import jax, jax.numpy as jnp
        import numpy as np
        B, S, H = (8, 128, 128)
        FF = 512
        E = 8
        TOP_K = 2
        LN_EPS = 1e-12

        def _layernorm(x, w, b):
            mu = jnp.mean(x, axis=-1, keepdims=True)
            var = jnp.mean(jnp.square(x - mu), axis=-1, keepdims=True)
            return (x - mu) * jax.lax.rsqrt(var + LN_EPS) * w + b
        key = jax.random.key(seed)
        ks = jax.random.split(key, 8)
        sc_h = 1.0 / np.sqrt(H)
        sc_ff = 1.0 / np.sqrt(FF)
        return {'hidden_states': jax.random.normal(ks[0], (B, S, H), jnp.float32), 'router_w': jax.random.normal(ks[1], (E, H), jnp.float32) * sc_h, 'router_b': jnp.zeros((E,), jnp.float32), 'w1': jax.random.normal(ks[2], (E, FF, H), jnp.float32) * sc_h, 'b1': jax.random.normal(ks[3], (E, FF), jnp.float32) * 0.01, 'w2': jax.random.normal(ks[4], (E, H, FF), jnp.float32) * sc_ff, 'b2': jax.random.normal(ks[5], (E, H), jnp.float32) * 0.01, 'ln_w': jnp.ones((H,), jnp.float32), 'ln_b': jnp.zeros((H,), jnp.float32)}
    _L0_ffn_all = _L0_ffn_setup()
    _L0_ffn_in = {k: v for k, v in _L0_ffn_all.items() if k in ('router_w', 'router_b', 'w1', 'b1', 'w2', 'b2', 'ln_w', 'ln_b')}
    del _L0_ffn_all
    return {'x': x, 'ctx_2048': ctx_2048, 'L0_xattn_Wq': _L0_xattn_in['Wq'], 'L0_xattn_Wkv': _L0_xattn_in['Wkv'], 'L0_xattn_null_kv': _L0_xattn_in['null_kv'], 'L0_xattn_Wout': _L0_xattn_in['Wout'], 'L0_xattn_ln_scale': _L0_xattn_in['ln_scale'], 'L0_xattn_ln_bias': _L0_xattn_in['ln_bias'], 'L0_ffn_router_w': _L0_ffn_in['router_w'], 'L0_ffn_router_b': _L0_ffn_in['router_b'], 'L0_ffn_w1': _L0_ffn_in['w1'], 'L0_ffn_b1': _L0_ffn_in['b1'], 'L0_ffn_w2': _L0_ffn_in['w2'], 'L0_ffn_b2': _L0_ffn_in['b2'], 'L0_ffn_ln_w': _L0_ffn_in['ln_w'], 'L0_ffn_ln_b': _L0_ffn_in['ln_b']}

def reference(x, ctx_2048, L0_xattn_Wq, L0_xattn_Wkv, L0_xattn_null_kv, L0_xattn_Wout, L0_xattn_ln_scale, L0_xattn_ln_bias, L0_ffn_router_w, L0_ffn_router_b, L0_ffn_w1, L0_ffn_b1, L0_ffn_w2, L0_ffn_b2, L0_ffn_ln_w, L0_ffn_ln_b):
    import jax
    import jax.numpy as jnp

    def _L0_xattn_ref(x, context, Wq, Wkv, null_kv, Wout, ln_scale, ln_bias):
        import jax, jax.numpy as jnp
        import numpy as np
        B, N, DIM = (8, 512, 128)
        M, CTX = (32, 256)
        HEADS, DH = (16, 64)
        INNER = HEADS * DH
        EPS = 1e-06

        def _split_heads(t):
            b, n, _ = t.shape
            return t.reshape(b, n, HEADS, DH).transpose(0, 2, 1, 3)
        scale = DH ** (-0.5)
        b = x.shape[0]
        q = _split_heads(jnp.einsum('bnd,df->bnf', x, Wq))
        kv = jnp.einsum('bmc,cf->bmf', context, Wkv)
        k, v = jnp.split(kv, 2, axis=-1)
        k, v = (_split_heads(k), _split_heads(v))
        nk = jnp.broadcast_to(null_kv[0], (b, HEADS, 1, DH))
        nv = jnp.broadcast_to(null_kv[1], (b, HEADS, 1, DH))
        k = jnp.concatenate((nk, k), axis=-2)
        v = jnp.concatenate((nv, v), axis=-2)
        q = q * scale
        sim = jnp.einsum('bhid,bhjd->bhij', q, k)
        attn = jax.nn.softmax(sim, axis=-1)
        out = jnp.einsum('bhij,bhjd->bhid', attn, v)
        out = out.transpose(0, 2, 1, 3).reshape(b, -1, INNER)
        out = jnp.einsum('bnf,fd->bnd', out, Wout)
        mu = jnp.mean(out, axis=-1, keepdims=True)
        var = jnp.var(out, axis=-1, keepdims=True)
        out = (out - mu) * jax.lax.rsqrt(var + EPS) * ln_scale + ln_bias
        return out

    def _L0_ffn_ref(hidden_states, router_w, router_b, w1, b1, w2, b2, ln_w, ln_b):
        import jax, jax.numpy as jnp
        import numpy as np
        B, S, H = (8, 128, 128)
        FF = 512
        E = 8
        TOP_K = 2
        LN_EPS = 1e-12

        def _layernorm(x, w, b):
            mu = jnp.mean(x, axis=-1, keepdims=True)
            var = jnp.mean(jnp.square(x - mu), axis=-1, keepdims=True)
            return (x - mu) * jax.lax.rsqrt(var + LN_EPS) * w + b
        b, s, h = hidden_states.shape
        flat = hidden_states.reshape(-1, h)
        logits = flat @ router_w.T + router_b
        topk_vals, topk_idx = jax.lax.top_k(logits, TOP_K)
        topk_w = jax.nn.softmax(topk_vals, axis=-1)
        out = jnp.zeros_like(flat)
        n_exp = w1.shape[0]
        for e in range(n_exp):
            cw = jnp.sum(jnp.where(topk_idx == e, topk_w, 0.0), axis=-1)
            y = jax.nn.gelu(flat @ w1[e].T + b1[e], approximate=False)
            y = y @ w2[e].T + b2[e]
            out = out + y * cw[:, None]
        out = out.reshape(b, s, h) + hidden_states
        return _layernorm(out, ln_w, ln_b)
    x = x + _L0_xattn_ref(_layernorm(x, axis=-1), ctx_2048, L0_xattn_Wq, L0_xattn_Wkv, L0_xattn_null_kv, L0_xattn_Wout, L0_xattn_ln_scale, L0_xattn_ln_bias)
    x = x + _L0_ffn_ref(_layernorm(x, axis=-1), L0_ffn_router_w, L0_ffn_router_b, L0_ffn_w1, L0_ffn_b1, L0_ffn_w2, L0_ffn_b2, L0_ffn_ln_w, L0_ffn_ln_b)
    return x

_drawn_inputs = setup_inputs


def setup_inputs(seed=0):
    import zlib

    import numpy as np

    out = dict(_drawn_inputs(seed))
    spreads = {'L0_xattn_ln_scale': (1.0, 0.2),
     'L0_xattn_ln_bias': (0.0, 0.1),
     'L0_ffn_router_b': (0.0, 0.1),
     'L0_ffn_ln_w': (1.0, 0.2),
     'L0_ffn_ln_b': (0.0, 0.1)}
    factors = {'L0_xattn_null_kv': 6.541, 'L0_ffn_b1': 27.712, 'L0_ffn_b2': 8.0}
    for name, (base, spread) in spreads.items():
        noise = np.random.default_rng([zlib.crc32(name.encode()), seed]).standard_normal(out[name].shape)
        drawn = base * np.exp(spread * noise) if base else spread * noise
        out[name] = jnp.asarray(drawn.astype(out[name].dtype))
    for name, factor in factors.items():
        out[name] = (out[name] * factor).astype(out[name].dtype)
    return out
```

```python
import math
from contextlib import ExitStack

import concourse.bass as bass
from concourse import mybir

F32 = mybir.dt.float32
F32R = mybir.dt.float32r
U32 = mybir.dt.uint32
ALU = mybir.AluOpType
ACT = mybir.ActivationFunctionType
AX = mybir.AxisListType

P = 128
B, N, DIM = 4, 256, 128
M, CTX = 256, 256
HEADS, DH = 16, 64
INNER = HEADS * DH
PAIRS = HEADS // 2
UNITS = PAIRS
QT = N // P
KT = M // P
CK = CTX // P
TOK = B * N
TILES = TOK // P
E, FF = 8, 512
FC = FF // P
CH = 512
CHUNKS = TOK // CH
CT = CH // P
VP = 4
SCALE = DH ** -0.5
NORMS = 2
EPS_PRE, EPS_ATT, EPS_MOE = 1e-5, 1e-6, 1e-12
ROWS = 4 * DIM + E + DH
COLS = E * FC + 2 * E + 1
SPLIT = ((0, 0), (0, 1), (1, 0))


def build(nc, x, ctx_t, wq, wk, wv, wout, rows, columns, w1_t, w2_t, out):
    stack = ExitStack()
    with stack:
        def sb(name, shape, dt=F32):
            return stack.enter_context(nc.sbuf_tensor(name, shape, dt))

        def sem(name):
            return stack.enter_context(nc.semaphore(name))

        x_sb = sb("x_sb", [P, TILES, DIM])
        xn = sb("xn", [P, TILES, DIM])
        x1 = xn
        xnT = sb("xnT", [P, 2, TOK], F32R)
        wq_s = sb("wq_s", [P, 2, INNER], F32R)
        wk_s = sb("wk_s", [P, 2, CK, INNER], F32R)
        wv_s = sb("wv_s", [P, 2, CK, INNER], F32R)
        wout_s = sb("wout_s", [P, 2, PAIRS, DIM], F32R)
        ctxT = sb("ctxT", [P, 2, CK, TOK], F32R)
        ctxV = sb("ctxV", [P, 2, CK, M], F32R)
        QK = sb("QK", [P, 2, UNITS, N + M], F32R)
        Hs = QK
        V = sb("V", [P, KT, INNER])
        Hf = V[:, :, :].rearrange("p k (f n) -> p (k f) n", n=CH)
        wq_raw = V[:, 0, :]
        Pr = sb("Pr", [P, 2, 2, QT, M])
        ctx_raw = Pr[:, :, :, :, :].rearrange("p a h t m -> p (a h t m)").rearrange("p (k n) -> p k n", k=CK)
        cwB = Pr[:, 0, :, :, :].rearrange("p h t m -> p (h t m)").rearrange("p (s n) -> p s n", s=2)
        PT = sb("PT", [P, 2, 2, KT * N])
        wk_raw = PT[:, :, :, :].rearrange("p a h n -> p (a h n)").rearrange("p (k n) -> p k n", k=CK)
        O = sb("O", [P, 2, UNITS, N], F32R)
        y_att = sb("y_att", [P, TILES, DIM])
        yT = sb("yT", [P, TOK])
        xn2 = sb("xn2", [P, TILES, DIM])
        xn2T = sb("xn2T", [P, 2, TOK], F32R)
        Wraw = sb("Wraw", [P, 2, 2, FF])
        wv_raw = Wraw[:, :, :, :].rearrange("p s w n -> p (s w n)").rearrange("p (k n) -> p k n", k=CK)
        Ws = wk_s
        acc = sb("acc", [P, TOK])
        wout_raw = acc[:, :].rearrange("p (c n) -> p c n", c=PAIRS)
        tmp = sb("tmp", [P, CH])
        ident = sb("ident", [P, P])
        rows_b = sb("rows_b", [P, ROWS])
        l1w, l1b, l2w, l2b = (rows_b[:, i * DIM:(i + 1) * DIM] for i in range(4))
        rb_b, nk_b = rows_b[:, 4 * DIM:4 * DIM + E], rows_b[:, 4 * DIM + E:ROWS]
        cols_sb = sb("cols_sb", [P, COLS])
        b1_sb, b2_sb, rw_f, nv_col = (cols_sb[:, a:b] for a, b in ((0, E * FC), (E * FC, E * FC + E),
                                                                   (E * FC + E, E * FC + 2 * E), (COLS - 1, COLS)))
        NVB = sb("NVB", [P, PAIRS, HEADS])
        NKf = sb("NKf", [P, HEADS])
        NK_s = sb("NK_s", [P, 2, HEADS], F32R)
        NW = sb("NW", [HEADS, DIM])
        nsn = sb("nsn", [P, TILES, HEADS])
        pn = sb("pn", [P, TILES, HEADS])
        pnT = sb("pnT", [HEADS, CH])
        mx = sb("mx", [P, 4, 4])
        nm = sb("nm", [P, 4, 4])
        t4 = sb("t4", [P, 4, 4])
        en = sb("en", [P, 4, 4])
        sm = sb("sm", [P, 4, 4])
        den = sb("den", [P, 4, 4])
        rden = sb("rden", [P, 4, 4])
        st = sb("st", [P, TILES, 6])
        mv = sb("mv", [P, TILES, 2])
        ve = sb("ve", [P, TILES])
        rstd = sb("rstd", [P, TILES])
        mhalf = sb("mhalf", [P, TILES])
        euler = sb("euler", [P, CT])
        iota8 = sb("iota8", [P, E])
        rw_s = sb("rw_s", [P, 2, E], F32R)
        lg = sb("lg", [P, CT, E])
        top = sb("top", [P, CT, E])
        topi = sb("topi", [P, CT, E], U32)
        topf = sb("topf", [P, CT, E])
        gd = sb("gd", [P, CT])
        ge = sb("ge", [P, CT])
        g1 = sb("g1", [P, CT])
        gw0 = sb("gw0", [P, CT])
        gw1 = sb("gw1", [P, CT])
        ca = sb("ca", [P, CT, E])
        cb = sb("cb", [P, CT, E])
        cw = sb("cw", [P, CT, E])
        cwT = sb("cwT", [E, CH])
        cw_dram = nc.dram_tensor("cw_scratch", (E, TOK), F32, kind="Internal").ap()

        S = stack.enter_context(nc.psum_tensor("S", [P, 2, 2, QT * M], F32))
        Tb = stack.enter_context(nc.psum_tensor("Tb", [P, 2, KT * N], F32))
        Ob = stack.enter_context(nc.psum_tensor("Ob", [P, 512], F32))
        Rb = stack.enter_context(nc.psum_tensor("Rb", [P, 512], F32))
        lead_banks = [Tb[:, 0, :], Tb[:, 1, :], Ob[:, :], Rb[:, :]]
        xn_banks = [S[:, i // 2, i % 2, 0:N] for i in range(4)]
        Hb = [S[:, 0, 0, :], S[:, 0, 1, :], S[:, 1, 0, :], S[:, 1, 1, :]]
        Yb = [Tb[:, 0, :], Tb[:, 1, :]]

        ld_x0, ld_x, ld_wq, ld_ctx0, ld_ctx1, ld_wk, ld_wv, ld_wout, ld_small = (
            sem(n) for n in ("ld_x0", "ld_x", "ld_wq", "ld_ctx0", "ld_ctx1", "ld_wk", "ld_wv", "ld_wout", "ld_small"))
        ident_ok, const_ok = sem("ident_ok"), sem("const_ok")
        var_ok, rstd_ok, xn_ok = sem("var_ok"), sem("rstd_ok"), sem("xn_ok")
        xnT_mm, xnT_hi, xnT_lo = sem("xnT_mm"), sem("xnT_hi"), sem("xnT_lo")
        wq_hi, wq_lo, wk_hi, wk_lo, wv_hi, wv_lo = (sem(n) for n in ("wq_hi", "wq_lo", "wk_hi", "wk_lo", "wv_hi", "wv_lo"))
        ctx0_hi, ctx0_lo, ctx1_hi, ctx1_lo, wout_hi, wout_lo, ctxV_ok = (
            sem(n) for n in ("ctx0_hi", "ctx0_lo", "ctx1_hi", "ctx1_lo", "wout_hi", "wout_lo", "ctxV_ok"))
        nk_prod, nk_lo, ns_mm, ns_ok = (sem(n) for n in ("nk_prod", "nk_lo", "ns_mm", "ns_ok"))
        qk_mm, qk_hi, qk_lo = sem("qk_mm"), sem("qk_hi"), sem("qk_lo")
        v_mm, v_sb = sem("v_mm"), sem("v_sb")
        s_done, mx_ok, nm_ok, t4_ok, exp_done = (sem(n) for n in ("s_done", "mx_ok", "nm_ok", "t4_ok", "exp_done"))
        den_ok, rden_ok, pn_ok, scaled = (sem(n) for n in ("den_ok", "rden_ok", "pn_ok", "scaled"))
        t_done, pt_sb, pt_sb2, pv_done, o_hi, o_lo = (sem(n) for n in ("t_done", "pt_sb", "pt_sb2", "pv_done", "o_hi", "o_lo"))
        out_mm, y_sb = sem("out_mm"), sem("y_sb")
        nvb_ok, nw_mm, nw_sb, pnT_mm, pnT_sb, null_mm, x1_ok, xn2_ok, xn2T_mm, xn2T_hi, xn2T_lo, y_full, y_mm = (
            sem(n) for n in ("nvb_ok", "nw_mm", "nw_sb", "pnT_mm", "pnT_sb", "null_mm", "x1_ok", "xn2_ok", "xn2T_mm", "xn2T_hi", "xn2T_lo", "y_full", "y_mm"))
        rw_lo, lg_mm, lg_ok, gap_ok, ge_ok, cw_ok, cwT_mm, cwT_ok, accT_mm, res_ok, dve_link, h_hi3 = (
            sem(n) for n in ("rw_lo", "lg_mm", "lg_ok", "gap_ok", "ge_ok", "cw_ok", "cwT_mm", "cwT_ok", "accT_mm", "res_ok", "dve_link", "h_hi3"))
        acc_zero, xb_ok = sem("acc_zero"), sem("xb_ok")
        cw_st, cwB_ok = sem("cw_st"), [sem("cwB_ok0"), sem("cwB_ok1")]
        wraw_ok, wsplit = [sem("wraw_ok0"), sem("wraw_ok1")], sem("wsplit")
        w1_done, gelu_done, h_hi, h_lo, w2_done, y_part, y_done = (
            sem(n) for n in ("w1_done", "gelu_done", "h_hi", "h_lo", "w2_done", "y_part", "y_done"))
        store = sem("store")
        pool_past, act_past = sem("pool_past"), sem("act_past")

        block = stack.enter_context(nc.Block())

        @block.sync
        def _(sp):
            sp.dma_start(x_sb[:, 0:QT, :], x[:, 0:QT, :]).then_inc(ld_x0, 16)
            sp.dma_start(wq_raw, wq).then_inc(ld_wq, 16)
            sp.dma_start(ctx_raw[:, :, 0:M], ctx_t[:, :, 0:M]).then_inc(ld_ctx0, 16)
            sp.dma_start(wk_raw, wk).then_inc(ld_wk, 16)
            sp.dma_start(x_sb[:, QT:TILES, :], x[:, QT:TILES, :]).then_inc(ld_x, 16)
            sp.dma_start(ctx_raw[:, :, M:TOK], ctx_t[:, :, M:TOK]).then_inc(ld_ctx1, 16)
            sp.dma_start(wv_raw, wv).then_inc(ld_wv, 16)
            sp.dma_start(wout_raw, wout).then_inc(ld_wout, 16)

            def load_expert(e, s):
                sp.dma_start(Wraw[:, s, 0, :], w1_t[bass.ds(e, 1), :, :].rearrange("e p n -> p (e n)")).then_inc(wraw_ok[s], 16)
                sp.dma_start(Wraw[:, s, 1, :], w2_t[bass.ds(e, 1), :, :].rearrange("e p n -> p (e n)")).then_inc(wraw_ok[s], 16)

            def gate(e, c, s):
                sp.dma_start(cwB[:, s, :], cw_dram[bass.ds(e, 1), c * CH:(c + 1) * CH].to_broadcast([P, CH])).then_inc(cwB_ok[s], 16)

            sp.wait_ge(wv_hi, 1)
            sp.wait_ge(wv_lo, 1)
            load_expert(0, 0)
            load_expert(1, 1)
            for c in range(CHUNKS):
                sp.wait_ge(cwT_ok, c + 1)
                sp.dma_start(cw_dram[:, c * CH:(c + 1) * CH], cwT[:, :]).then_inc(cw_st, 16)
                sp.wait_ge(cw_st, 16 * (c + 1))
                gate(0, c, c)

            def gates(k, i):
                sp.wait_ge(y_done, 4 * k + i + 3)
                gate(2 * k + (i + 2) // CHUNKS, i % CHUNKS, i % 2)

            with sp.Fori(0, E // 2 - 1) as k:
                for s in range(2):
                    sp.wait_ge(wsplit, 4 * (2 * k + s + 1))
                    load_expert(2 * k + s + 2, s)
                    gates(k, 2 * s)
                    gates(k, 2 * s + 1)
            for i in range(2):
                gates(E // 2 - 1, i)
            for c in range(CHUNKS):
                sp.wait_ge(res_ok, c + 1)
                sp.dma_start(out[:, c * CT:(c + 1) * CT, :], y_att[:, c * CT:(c + 1) * CT, :]).then_inc(store, 16)
            sp.wait_ge(store, 16 * CHUNKS)

        @block.gpsimd
        def _(pool):
            pool.memset(ident[:], 0.0).then_inc(ident_ok, 1)
            pool.wait_ge(ident_ok, 1)
            pool.affine_select(out=ident[:], in_=ident[:], compare_op=ALU.not_equal, fill=1.0, base=0,
                               pattern=[[-1, P]], channel_multiplier=1).then_inc(ident_ok, 1)
            pool.memset(mhalf[:], -0.5).then_inc(const_ok, 1)
            pool.memset(euler[:], math.e).then_inc(const_ok, 1)
            pool.iota(iota8[:], pattern=[[1, E]], base=0, channel_multiplier=0,
                      allow_small_or_imprecise_dtypes=True).then_inc(const_ok, 1)
            pool.memset(NVB[:], 0.0).then_inc(const_ok, 1)
            pool.wait_ge(const_ok, 1)
            pool.wait_ge(var_ok, 1)
            pool.tensor_tensor(rstd[:, 0:QT], ve[:, 0:QT], mhalf[:, 0:QT], ALU.pow).then_inc(rstd_ok, 1)
            pool.wait_ge(ld_wq, 16)
            pool.wait_ge(ld_small, 32)
            pool.tensor_tensor(y_att[:, :, :].rearrange("p t n -> p (t n)").rearrange("p (h d) -> p h d", d=DH),
                               wq_raw.rearrange("p (h d) -> p h d", d=DH),
                               nk_b[:, None, :].to_broadcast([P, HEADS, DH]), ALU.mult).then_inc(nk_prod, 1)
            pool.wait_ge(var_ok, 2)
            pool.tensor_tensor(rstd[:, QT:TILES], ve[:, QT:TILES], mhalf[:, QT:TILES], ALU.pow).then_inc(rstd_ok, 1)
            pool.wait_ge(ctx0_lo, 1)
            for r in range(2):
                pool.tensor_copy(ctxV[:, r, :, :], ctxT[:, r, :, 0:M]).then_inc(ctxV_ok, 1)
            pool.wait_ge(ld_ctx1, 16)
            pool.tensor_scalar(ctxT[:, 0, :, M:TOK], ctx_raw[:, :, M:TOK], 1.0, 1.0, ALU.mult, ALU.mult).then_inc(ctx1_hi, 1)
            pool.wait_ge(ctx1_hi, 1)
            pool.tensor_tensor(ctxT[:, 1, :, M:TOK], ctx_raw[:, :, M:TOK], ctxT[:, 0, :, M:TOK].bitcast(F32),
                               ALU.subtract).then_inc(ctx1_lo, 1)

            def scale(b, p):
                pool.wait_ge(rden_ok, UNITS * b + p + 1)
                pool.sem_inc(pool_past, 1)
                for h in range(2):
                    for q in range(QT):
                        last = pool.tensor_scalar(Pr[:, p % 2, h, q, :], Pr[:, p % 2, h, q, :],
                                                  rden[:, p % 4, h * QT + q:h * QT + q + 1], 1.0, ALU.mult, ALU.mult)
                last.then_inc(scaled, 1)

            scale(0, 0)
            scale(0, 1)
            pool.wait_ge(ld_wout, 16)
            pool.tensor_scalar(wout_s[:, 0, :, :], wout_raw, 1.0, 1.0, ALU.mult, ALU.mult).then_inc(wout_hi, 1)
            pool.wait_ge(wout_hi, 1)
            pool.tensor_tensor(wout_s[:, 1, :, :], wout_raw, wout_s[:, 0, :, :].bitcast(F32), ALU.subtract).then_inc(wout_lo, 1)

            def body(b, last):
                for p in range(UNITS):
                    if p + 2 < UNITS:
                        scale(b, p + 2)
                    elif not last:
                        scale(b + 1, p + 2 - UNITS)
                    if p == 0 and not last:
                        pool.wait_ge(v_mm, VP * (b + 1))
                        pool.sem_inc(pool_past, 1)
                        for r in range(2):
                            pool.tensor_copy(ctxV[:, r, :, :], ctxT[:, r, :, bass.ds((b + 1) * M, M)]).then_inc(ctxV_ok, 1)

            with pool.Fori(0, B - 1) as b:
                body(b, False)
            body(B - 1, True)

            def split(e, s):
                for w in range(2):
                    hi, lo = (Ws[:, r, s, w * FF:(w + 1) * FF] for r in range(2))
                    pool.tensor_scalar(hi, Wraw[:, s, w, :], 1.0, 1.0, ALU.mult, ALU.mult).then_inc(wsplit, 1)
                    pool.wait_ge(wsplit, 4 * e + 2 * w + 1)
                    pool.tensor_tensor(lo, Wraw[:, s, w, :], hi.bitcast(F32), ALU.subtract).then_inc(wsplit, 1)

            pool.wait_ge(qk_mm, UNITS * B)
            for e in range(2):
                pool.wait_ge(wraw_ok[e], 32)
                split(e, e)
            pool.tensor_tensor(x_sb[:], x_sb[:], l1b[:, None, :].to_broadcast([P, TILES, DIM]), ALU.add).then_inc(xb_ok, 1)
            pool.wait_ge(nw_mm, 1)
            pool.memset(acc[:], 0.0).then_inc(acc_zero, 1)
            for c in range(CHUNKS):
                t = slice(c * CT, (c + 1) * CT)
                for n in range(2):
                    pool.wait_ge(var_ok, NORMS + 2 * c + n + 1)
                    pool.tensor_tensor(rstd[:, t], ve[:, t], mhalf[:, t], ALU.pow).then_inc(rstd_ok, 1)
                pool.wait_ge(gap_ok, c + 1)
                pool.tensor_tensor(ge[:], euler[:], gd[:], ALU.pow).then_inc(ge_ok, 1)
            pool.wait_ge(x1_ok, CHUNKS)
            pool.wait_ge(xn2_ok, CHUNKS)
            pool.tensor_tensor(x_sb[:], x1[:], l2b[:, None, :].to_broadcast([P, TILES, DIM]), ALU.add).then_inc(xb_ok, 1)
            with pool.Fori(1, E // 2) as k:
                for s in range(2):
                    pool.wait_ge(w2_done, 4 * k + 2 * s - 1)
                    pool.wait_ge(wraw_ok[s], 32 * (k + 1))
                    pool.sem_inc(pool_past, 1)
                    split(2 * k + s, s)
            for c in range(CHUNKS):
                t = slice(c * CT, (c + 1) * CT)
                pool.wait_ge(var_ok, NORMS + 2 * CHUNKS + c + 1)
                pool.tensor_tensor(rstd[:, t], ve[:, t], mhalf[:, t], ALU.pow).then_inc(rstd_ok, 1)

        @block.scalar
        def _(act):
            act.sem_inc(y_sb, 1)
            act.dma_start(rows_b[:], rows.to_broadcast([P, ROWS])).then_inc(ld_small, 16)
            act.dma_start(cols_sb[:], columns).then_inc(ld_small, 16)
            act.wait_ge(ld_wq, 16)
            act.activation(wq_s[:, 0, :], wq_raw, ACT.Copy).then_inc(wq_hi, 1)
            act.wait_ge(ld_ctx0, 16)
            act.activation(ctxT[:, 0, :, 0:M], ctx_raw[:, :, 0:M], ACT.Copy).then_inc(ctx0_hi, 1)
            act.wait_ge(xnT_mm, 1)
            act.activation(xnT[:, 0, 0:N], xn_banks[0], ACT.Copy).then_inc(xnT_hi, 1)
            act.wait_ge(ld_wk, 16)
            act.activation(wk_s[:, 0, :, :], wk_raw, ACT.Copy).then_inc(wk_hi, 1)

            def xnT_part(g):
                act.wait_ge(xnT_mm, g + 1)
                act.activation(xnT[:, 0, g * N:(g + 1) * N], xn_banks[g], ACT.Copy).then_inc(xnT_hi, 1)

            def qk_part(b, c, bank):
                act.wait_ge(qk_mm, UNITS * b + c + 1)
                act.activation(QK[:, 0, c, :], bank, ACT.Copy).then_inc(qk_hi, 1)

            def exps(b, p, u):
                act.wait_ge(t4_ok, UNITS * b + p + 1)
                act.activation(en[:, p % 4, :], t4[:, p % 4, :], ACT.Exp)
                if not (isinstance(u, int) and u < 2):
                    act.wait_ge(t_done, UNITS * b + p - 1)
                for h in range(2):
                    for q in range(QT):
                        i = h * QT + q
                        last = act.activation(Pr[:, p % 2, h, q, :], S[:, p % 2, h, q * M:(q + 1) * M], ACT.Exp,
                                              bias=nm[:, p % 4, i:i + 1], scale=SCALE,
                                              accum_out=sm[:, p % 4, i:i + 1])
                last.then_inc(exp_done, 1)

            def values(b, i, bank):
                half, kt = i // 2, i % 2
                act.wait_ge(v_mm, VP * b + i + 1)
                if half and not (isinstance(b, int) and b == 0):
                    act.wait_ge(pv_done, UNITS * b)
                act.activation(V[:, kt, half * 512:(half + 1) * 512], bank, ACT.Copy).then_inc(v_sb, 1)

            def probabilities(b, p):
                act.wait_ge(t_done, UNITS * b + p + 1)
                act.activation(PT[:, p % 2, 1, :], Tb[:, 1, :], ACT.Copy).then_inc(pt_sb2, 1)

            def o_part(b, p):
                act.wait_ge(pv_done, UNITS * b + p + 1)
                act.activation(O[:, 0, p, :], Ob[:, 0:N], ACT.Copy).then_inc(o_hi, 1)

            for c in range(3):
                qk_part(0, c, lead_banks[c])
            for g in range(1, B):
                xnT_part(g)
            qk_part(0, 3, lead_banks[3])
            act.wait_ge(ctx1_lo, 1)
            qk_part(0, 4, lead_banks[0])
            exps(0, 0, 0)
            qk_part(0, 5, lead_banks[1])
            qk_part(0, 6, lead_banks[2])
            qk_part(0, 7, lead_banks[3])
            act.wait_ge(ld_wv, 16)
            act.activation(wv_s[:, 0, :, :], wv_raw, ACT.Copy).then_inc(wv_hi, 1)
            exps(0, 1, 1)
            act.wait_ge(wq_lo, 1)
            act.wait_ge(nk_prod, 1)
            values(0, 0, lead_banks[0])
            values(0, 1, lead_banks[1])
            values(0, 2, lead_banks[2])
            values(0, 3, lead_banks[3])
            probabilities(0, 0)
            exps(0, 2, 2)

            def body(b, last):
                for p in range(UNITS):
                    if not last:
                        qk_part(b + 1, p, Rb[:, :])
                    if p + 3 < UNITS:
                        exps(b, p + 3, None)
                    elif not last:
                        exps(b + 1, p + 3 - UNITS, None)
                    if not last and p in (4, 5):
                        values(b + 1, p - 4, Rb[:, :])
                    if p + 1 < UNITS:
                        probabilities(b, p + 1)
                    elif not last:
                        probabilities(b + 1, 0)
                    o_part(b, p)
                if not last:
                    values(b + 1, 2, Rb[:, :])
                    values(b + 1, 3, Rb[:, :])
                act.wait_ge(out_mm, b + 1)
                act.sem_inc(act_past, 1)
                act.activation(yT[:, bass.ds(N * b, N)], Rb[:, 0:N], ACT.Copy).then_inc(y_sb, 1)

            with act.Fori(0, B - 1) as b:
                body(b, False)
            body(B - 1, True)

            def gelus(k, i):
                for f in range(FC):
                    act.wait_ge(w1_done, 16 * k + 4 * i + f + 1)
                    if not (isinstance(k, int) and 4 * k + i == 0):
                        act.wait_ge(h_lo, 16 * k + 4 * (i - 1) + f + 1)
                    act.sem_inc(act_past, 1)
                    act.activation(Hf[:, f, :], Hb[f], ACT.Gelu,
                                   bias=b1_sb[:, bass.ds(2 * FC * k + (i // CHUNKS) * FC + f, 1)]).then_inc(gelu_done, 1)
                    if f < FC - 1:
                        if f == 0 and not (isinstance(k, int) and 4 * k + i == 0):
                            act.wait_ge(w2_done, 4 * k + i)
                        act.wait_ge(gelu_done, 16 * k + 4 * i + f + 1)
                        act.activation(Hs[:, 0, (i % 2) * FC + f, :], Hf[:, f, :], ACT.Copy).then_inc(h_hi, 1)

            for c in range(CHUNKS):
                act.wait_ge(xn2T_mm, c + 1)
                act.activation(xn2T[:, 0, c * CH:(c + 1) * CH], Ob[:, :], ACT.Copy).then_inc(xn2T_hi, 1)
                if c == 0:
                    gelus(0, 0)
            with act.Fori(0, E // 2 - 1) as k:
                for i in range(1, 5):
                    gelus(k, i)
            for i in range(1, 4):
                gelus(E // 2 - 1, i)

        @block.tensor
        def _(pe):
            pe.sem_inc(w2_done, 1)

            def products(dst, left, right):
                steps = [(a[0 + x_], b_[0 + y_]) for a, b_ in zip(left, right) for x_, y_ in SPLIT]
                for n, (a, b_) in enumerate(steps):
                    last = pe.matmul(dst, a, b_, start=n == 0, stop=n == len(steps) - 1)
                return last

            def qk(b, c, bank):
                cols = slice(c * P, (c + 1) * P)
                products(bank[:, 0:N], [[wq_s[:, r, cols] for r in range(2)]],
                         [[xnT[:, r, bass.ds(b * N, N)] for r in range(2)]])
                products(bank[:, N:N + M], [[wk_s[:, r, k, cols] for r in range(2)] for k in range(CK)],
                         [[ctxT[:, r, k, bass.ds(b * M, M)] for r in range(2)] for k in range(CK)]).then_inc(qk_mm, 1)

            def value(b, i, bank):
                half, kt = i // 2, i % 2
                if i == 0:
                    pe.wait_ge(ctxV_ok, 2 * (b + 1))
                products(bank, [[ctxV[:, r, k, kt * P:(kt + 1) * P] for r in range(2)] for k in range(CK)],
                         [[wv_s[:, r, k, half * 512:(half + 1) * 512] for r in range(2)] for k in range(CK)]).then_inc(v_mm, 1)

            def scores(b, p, u):
                pe.wait_ge(qk_lo, UNITS * b + p + 1)
                if not (isinstance(u, int) and u < 2):
                    pe.wait_ge(exp_done, UNITS * b + p - 1)
                for q in range(QT):
                    for n, (i, j) in enumerate(SPLIT):
                        for h in range(2):
                            rows = slice(h * DH, (h + 1) * DH)
                            last = pe.matmul(S[:, p % 2, h, q * M:(q + 1) * M], QK[rows, i, p, q * P:(q + 1) * P],
                                             QK[rows, j, p, N:N + M], start=n == 0, stop=n == len(SPLIT) - 1)
                last.then_inc(s_done, 1)

            def transposes(b, p, u):
                pe.wait_ge(scaled, UNITS * b + p + 1)
                if not (isinstance(u, int) and u < 1):
                    pe.wait_ge(pt_sb, UNITS * b + p)
                    pe.wait_ge(pt_sb2, UNITS * b + p)
                for h in range(2):
                    for q in range(QT):
                        for k in range(KT):
                            last = pe.transpose(Tb[:, h, k * N + q * P:k * N + (q + 1) * P],
                                                Pr[:, p % 2, h, q, k * P:(k + 1) * P], ident[:, :])
                last.then_inc(t_done, 1)

            def attend(b, p):
                pe.wait_ge(pt_sb, UNITS * b + p + 1)
                pe.wait_ge(pt_sb2, UNITS * b + p + 1)
                pe.wait_ge(v_sb, VP * b + (2 if p < UNITS // 2 else 4))
                pe.wait_ge(o_lo, UNITS * b + p + 1)
                for k in range(KT):
                    for h in range(2):
                        head = 2 * p + h
                        last = pe.matmul(Ob[h * DH:(h + 1) * DH, 0:N], V[:, k, head * DH:(head + 1) * DH],
                                         PT[:, p % 2, h, k * N:(k + 1) * N], start=k == 0, stop=k == KT - 1)
                last.then_inc(pv_done, 1)

            def x_transposed(g):
                for t in range(QT * g, QT * (g + 1)):
                    pe.wait_ge(xn_ok, t + 1)
                    last = pe.transpose(xn_banks[g][:, (t % QT) * P:(t % QT + 1) * P], xn[:, t, :], ident[:, :])
                last.then_inc(xnT_mm, 1)

            def null_keys(ts):
                for t in ts:
                    last = products(Rb[:, t * HEADS:(t + 1) * HEADS],
                                    [[xnT[:, r, t * P:(t + 1) * P] for r in range(2)]], [[NK_s[:, r, :] for r in range(2)]])
                last.then_inc(ns_mm, 1)

            pe.wait_ge(ident_ok, 2)
            x_transposed(0)
            pe.wait_ge(wq_lo, 1)
            pe.wait_ge(xnT_lo, 1)
            pe.wait_ge(ctx0_lo, 1)
            pe.wait_ge(wk_lo, 1)
            for c in range(3):
                qk(0, c, lead_banks[c])
            pe.wait_ge(nk_lo, 1)
            null_keys(range(QT))
            for g in range(1, B):
                x_transposed(g)
            pe.wait_ge(xnT_lo, 2)
            scores(0, 0, 0)
            pe.wait_ge(ns_ok, 1)
            qk(0, 3, lead_banks[3])
            pe.wait_ge(qk_lo, 1)
            qk(0, 4, lead_banks[0])
            pe.wait_ge(xnT_lo, B)
            scores(0, 1, 1)
            for c in range(5, UNITS):
                pe.wait_ge(qk_lo, c - 3)
                qk(0, c, lead_banks[c - 4])
            pe.wait_ge(qk_lo, UNITS)
            null_keys(range(QT, TILES))
            pe.wait_ge(wv_lo, 1)
            for i in range(VP):
                pe.wait_ge(qk_lo, 5 + i)
                if i == VP - 1:
                    pe.wait_ge(ns_ok, 2)
                value(0, i, lead_banks[i])
                if i == 1:
                    scores(0, 2, 2)
            pe.wait_ge(v_sb, VP)
            transposes(0, 0, 0)

            def body(b, last):
                for p in range(UNITS):
                    if p + 3 < UNITS:
                        scores(b, p + 3, None)
                    elif not last:
                        scores(b + 1, p + 3 - UNITS, None)
                    if not last:
                        if p == 0:
                            pe.wait_ge(y_sb, b + 1)
                            pe.wait_ge(ctx1_lo, 1)
                        elif p in (5, 6):
                            pe.wait_ge(v_sb, VP * (b + 1) + p - 4)
                        else:
                            pe.wait_ge(qk_lo, UNITS * (b + 1) + p)
                        qk(b + 1, p, Rb)
                    if p + 1 < UNITS:
                        transposes(b, p + 1, None)
                    elif not last:
                        transposes(b + 1, 0, None)
                    if not last and p in (4, 5):
                        pe.wait_ge(qk_lo, UNITS * (b + 1) + p + 1)
                        value(b + 1, p - 4, Rb[:, :])
                    if not last and p == UNITS - 1:
                        pe.wait_ge(qk_lo, UNITS * (b + 2))
                        value(b + 1, 2, Rb[:, :])
                    attend(b, p)
                if not last:
                    pe.wait_ge(v_sb, VP * (b + 1) + 3)
                    value(b + 1, 3, Rb[:, :])
                    pe.wait_ge(v_sb, VP * (b + 2))
                pe.wait_ge(o_lo, UNITS * (b + 1) + 1)
                pe.wait_ge(wout_lo, 1)
                products(Rb[:, 0:N], [[wout_s[:, r, c, :] for r in range(2)] for c in range(PAIRS)],
                         [[O[:, r, c, :] for r in range(2)] for c in range(PAIRS)]).then_inc(out_mm, 1)

            with pe.Fori(0, B - 1) as b:
                body(b, False)
            body(B - 1, True)

            pe.wait_ge(nvb_ok, 2)
            pe.wait_ge(y_sb, B + 1)
            for c in range(PAIRS):
                last = pe.matmul(Rb[0:HEADS, 0:DIM], NVB[:, c, :], wout_raw[:, c, :], start=c == 0, stop=c == PAIRS - 1)
            last.then_inc(nw_mm, 1)

            def tail(c):
                pe.wait_ge(pn_ok, UNITS * B // CHUNKS * (c + 1))
                if c:
                    pe.wait_ge(cwT_ok, c)
                for t in range(CT):
                    last = pe.transpose(Ob[0:HEADS, t * P:(t + 1) * P], pn[:, c * CT + t, :], ident[:, :])
                last.then_inc(pnT_mm, 1)
                pe.wait_ge(pnT_sb, c + 1)
                pe.wait_ge(nw_sb, 1)
                if c:
                    pe.wait_ge(lg_ok, c)
                pe.matmul(Rb[:, :], NW[:, :], pnT[:, :], start=True, stop=True).then_inc(null_mm, 1)
                pe.wait_ge(y_full, c + 1)
                for t in range(CT):
                    last = pe.transpose(Rb[:, t * DIM:(t + 1) * DIM], yT[:, (c * CT + t) * P:(c * CT + t + 1) * P], ident[:, :])
                last.then_inc(y_mm, 1)
                pe.wait_ge(xn2_ok, c + 1)
                for t in range(CT):
                    last = pe.transpose(Ob[:, t * P:(t + 1) * P], xn2[:, c * CT + t, :], ident[:, :])
                last.then_inc(xn2T_mm, 1)
                pe.wait_ge(xn2T_lo, c + 1)
                for t in range(CT):
                    tok = slice((c * CT + t) * P, (c * CT + t + 1) * P)
                    last = products(Rb[:, t * E:(t + 1) * E], [[xn2T[:, r, tok] for r in range(2)]],
                                    [[rw_s[:, r, :] for r in range(2)]])
                last.then_inc(lg_mm, 1)
                pe.wait_ge(cw_ok, c + 1)
                for t in range(CT):
                    last = pe.transpose(Ob[0:E, t * P:(t + 1) * P], cw[:, t, :], ident[:, :])
                last.then_inc(cwT_mm, 1)

            def up(k, i):
                s, c = (i // CHUNKS) % 2, i % CHUNKS
                if c == 0:
                    pe.wait_ge(wsplit, 4 * (2 * k + i // CHUNKS) + 2)
                for f in range(FC):
                    if not (isinstance(k, int) and 4 * k + i == 0):
                        pe.wait_ge(gelu_done, 16 * k + 4 * (i - 1) + f + 1)
                    products(Hb[f], [[Ws[:, r, s, f * P:(f + 1) * P] for r in range(2)]],
                             [[xn2T[:, r, c * CH:(c + 1) * CH] for r in range(2)]]).then_inc(w1_done, 1)

            def down(k, i):
                s, c = (i // CHUNKS) % 2, i % CHUNKS
                if c == 0:
                    pe.wait_ge(wsplit, 4 * (2 * k + i // CHUNKS) + 4)
                pe.wait_ge(y_done, 4 * k + i + 1)
                for f in range(FC):
                    pe.wait_ge(h_lo, 16 * k + 4 * i + f + 1)
                    for n, (x_, y_) in enumerate(SPLIT):
                        last = pe.matmul(Yb[c], Ws[:, x_, s, FF + f * P:FF + (f + 1) * P], Hs[:, y_, (i % 2) * FC + f, :],
                                         start=f == 0 and n == 0, stop=f == FC - 1 and n == len(SPLIT) - 1)
                last.then_inc(w2_done, 1)

            tail(0)
            up(0, 0)
            tail(1)
            with pe.Fori(0, E // 2 - 1) as k:
                for i in range(4):
                    up(k, i + 1)
                    down(k, i)
            for i in range(4):
                if i < 3:
                    up(E // 2 - 1, i + 1)
                down(E // 2 - 1, i)
            for c in range(CHUNKS):
                pe.wait_ge(y_done, 2 * E + 2 - (CHUNKS - 1 - c))
                bank = (Ob, Rb)[c]
                for t in range(CT):
                    last = pe.transpose(bank[:, t * P:(t + 1) * P], acc[:, (c * CT + t) * P:(c * CT + t + 1) * P], ident[:, :])
                last.then_inc(accT_mm, 1)

        @block.vector
        def _(dve):
            links = [0]

            def link(ins):
                links[0] += 1
                ins.then_inc(dve_link, 1)
                dve.wait_ge(dve_link, links[0])

            dve.sem_inc(o_lo, 1)
            dve.sem_inc(y_done, 2)

            def lo_part(dst, full, hi):
                return dve.tensor_tensor(dst, full, hi.bitcast(F32), ALU.subtract)

            def statistics(src, ts, eps):
                for t in ts:
                    last = dve.bn_stats(st[:, t, :], src[:, t - ts[0], :])
                link(last)
                for t in ts:
                    last = dve.bn_aggr(mv[:, t, :], st[:, t, :])
                link(last)
                dve.tensor_scalar(ve[:, ts[0]:ts[-1] + 1], mv[:, ts[0]:ts[-1] + 1, 1], eps, None, ALU.add).then_inc(var_ok, 1)

            def normalize(dst, src, ts, n):
                dve.wait_ge(rstd_ok, n)
                for t in ts:
                    last = dve.tensor_scalar(dst[:, t - ts[0], :], src[:, t - ts[0], :], mv[:, t, 0:1], rstd[:, t:t + 1],
                                             ALU.subtract, ALU.mult)
                return last

            def normalized(ts, n):
                dve.wait_ge(rstd_ok, n)
                for t in ts:
                    dve.tensor_scalar(xn[:, t, :], x_sb[:, t, :], mv[:, t, 0:1], rstd[:, t:t + 1],
                                      ALU.subtract, ALU.mult).then_inc(xn_ok, 1)

            def xnT_part(g):
                dve.wait_ge(xnT_hi, g + 1)
                lo_part(xnT[:, 1, g * N:(g + 1) * N], xn_banks[g], xnT[:, 0, g * N:(g + 1) * N]).then_inc(xnT_lo, 1)

            def null_keys(ts):
                dve.wait_ge(ns_mm, 1 + (ts[0] > 0))
                dve.tensor_scalar(nsn[:, ts[0]:ts[-1] + 1, :].rearrange("p t h -> p (t h)"),
                                  Rb[:, ts[0] * HEADS:(ts[-1] + 1) * HEADS], -SCALE, None, ALU.mult).then_inc(ns_ok, 1)

            dve.wait_ge(ld_x0, 16)
            statistics(x_sb[:, 0:QT, :], list(range(QT)), EPS_PRE)
            dve.wait_ge(wq_hi, 1)
            lo_part(wq_s[:, 1, :], wq_raw, wq_s[:, 0, :]).then_inc(wq_lo, 1)
            normalized(range(QT), 1)
            dve.wait_ge(ctx0_hi, 1)
            lo_part(ctxT[:, 1, :, 0:M], ctx_raw[:, :, 0:M], ctxT[:, 0, :, 0:M]).then_inc(ctx0_lo, 1)
            xnT_part(0)
            dve.wait_ge(wk_hi, 1)
            lo_part(wk_s[:, 1, :, :], wk_raw, wk_s[:, 0, :, :]).then_inc(wk_lo, 1)
            dve.wait_ge(nk_prod, 1)
            link(dve.tensor_reduce(NKf[:], y_att[:, :, :].rearrange("p t n -> p (t n)").rearrange("p (h d) -> p h d", d=DH),
                                   AX.X, ALU.add))
            link(dve.tensor_copy(NK_s[:, 0, :], NKf[:]))
            lo_part(NK_s[:, 1, :], NKf[:], NK_s[:, 0, :]).then_inc(nk_lo, 1)
            dve.wait_ge(ld_x, 16)
            statistics(x_sb[:, QT:TILES, :], list(range(QT, TILES)), EPS_PRE)

            def qk_part(b, c, bank):
                dve.wait_ge(qk_hi, UNITS * b + c + 1)
                lo_part(QK[:, 1, c, :], bank, QK[:, 0, c, :]).then_inc(qk_lo, 1)

            def null_scores(src, b, p):
                return src[:, bass.ds(QT * b, QT), 2 * p:2 * p + 2].rearrange("p t h -> p h t")

            def by_head(small, p):
                return small[:, p % 4, :].rearrange("p (h t) -> p h t", h=2)

            def maxima(b, p):
                dve.wait_ge(s_done, UNITS * b + p + 1)
                dve.tensor_reduce(mx[:, p % 4, :], S[:, p % 2, :, :].rearrange("p h (t m) -> p (h t) m", m=M), AX.X, ALU.max,
                                  negate=True).then_inc(mx_ok, 1)
                dve.wait_ge(mx_ok, UNITS * b + p + 1)
                dve.scalar_tensor_tensor(by_head(nm, p), by_head(mx, p), SCALE, null_scores(nsn, b, p),
                                         ALU.mult, ALU.min).then_inc(nm_ok, 1)
                dve.wait_ge(nm_ok, UNITS * b + p + 1)
                dve.tensor_tensor(by_head(t4, p), by_head(nm, p), null_scores(nsn, b, p), ALU.subtract).then_inc(t4_ok, 1)

            def sums(b, p):
                dve.wait_ge(exp_done, UNITS * b + p + 1)
                dve.tensor_tensor(den[:, p % 4, :], sm[:, p % 4, :], en[:, p % 4, :], ALU.add).then_inc(den_ok, 1)
                dve.wait_ge(den_ok, UNITS * b + p + 1)
                dve.reciprocal(rden[:, p % 4, :], den[:, p % 4, :]).then_inc(rden_ok, 1)
                dve.wait_ge(rden_ok, UNITS * b + p + 1)
                dve.tensor_tensor(null_scores(pn, b, p), by_head(en, p), by_head(rden, p), ALU.mult).then_inc(pn_ok, 1)

            def probabilities(b, p):
                dve.wait_ge(t_done, UNITS * b + p + 1)
                dve.tensor_copy(PT[:, p % 2, 0, :], Tb[:, 0, :]).then_inc(pt_sb, 1)

            def o_part(b, p):
                dve.wait_ge(o_hi, UNITS * b + p + 1)
                lo_part(O[:, 1, p, :], Ob[:, 0:N], O[:, 0, p, :]).then_inc(o_lo, 1)

            qk_part(0, 0, lead_banks[0])
            normalized(range(QT, TILES), 2)
            qk_part(0, 1, lead_banks[1])
            qk_part(0, 2, lead_banks[2])
            null_keys(range(QT))
            xnT_part(1)
            maxima(0, 0)
            qk_part(0, 3, lead_banks[3])
            xnT_part(2)
            xnT_part(3)
            qk_part(0, 4, lead_banks[0])
            maxima(0, 1)
            for c in range(5, UNITS):
                qk_part(0, c, lead_banks[c - 4])
            null_keys(range(QT, TILES))
            dve.wait_ge(wv_hi, 1)
            lo_part(wv_s[:, 1, :, :], wv_raw, wv_s[:, 0, :, :]).then_inc(wv_lo, 1)
            sums(0, 0)
            maxima(0, 2)
            sums(0, 1)
            probabilities(0, 0)
            dve.wait_ge(const_ok, 4)
            for h in range(2):
                rows = slice(h * DH, (h + 1) * DH)
                flat = NVB[rows, :, :].rearrange("p c h -> p (c h)")
                dve.tensor_copy(flat[:, h:(PAIRS - 1) * (HEADS + 2) + h + 1:HEADS + 2],
                                nv_col[rows, 0:1].to_broadcast([DH, PAIRS])).then_inc(nvb_ok, 1)

            def body(b, last):
                for p in range(UNITS):
                    if p + 3 < UNITS:
                        maxima(b, p + 3)
                    elif not last:
                        maxima(b + 1, p + 3 - UNITS)
                    if p:
                        o_part(b, p - 1)
                    if p + 2 < UNITS:
                        sums(b, p + 2)
                    elif not last:
                        sums(b + 1, p + 2 - UNITS)
                    if not last:
                        qk_part(b + 1, p, Rb[:, :])
                    if p + 1 < UNITS:
                        probabilities(b, p + 1)
                    elif not last:
                        probabilities(b + 1, 0)
                o_part(b, UNITS - 1)

            with dve.Fori(0, B - 1) as b:
                body(b, False)
            body(B - 1, True)

            link(dve.tensor_copy(rw_s[:, 0, :], rw_f))
            lo_part(rw_s[:, 1, :], rw_f, rw_s[:, 0, :]).then_inc(rw_lo, 1)
            dve.wait_ge(nw_mm, 1)
            dve.tensor_copy(NW[:, :], Rb[0:HEADS, 0:DIM]).then_inc(nw_sb, 1)

            def over_rows(v):
                return v[:, None, :].to_broadcast([P, CT, DIM])

            def tail(c):
                t = slice(c * CT, (c + 1) * CT)
                ts = list(range(c * CT, (c + 1) * CT))
                tok = slice(c * CH, (c + 1) * CH)
                dve.wait_ge(pnT_mm, c + 1)
                dve.tensor_copy(pnT[:, :], Ob[0:HEADS, :]).then_inc(pnT_sb, 1)
                dve.wait_ge(null_mm, c + 1)
                dve.wait_ge(y_sb, B + 1)
                dve.tensor_tensor(yT[:, tok], yT[:, tok], Rb[:, :], ALU.add).then_inc(y_full, 1)
                y = Rb[:, :].rearrange("p (t n) -> p t n", t=CT)
                dve.wait_ge(y_mm, c + 1)
                statistics(y, ts, EPS_ATT)
                link(normalize(x1[:, t, :], y, ts, NORMS + 1 + 2 * c))
                link(dve.tensor_tensor(x1[:, t, :], x1[:, t, :], over_rows(l1w), ALU.mult))
                dve.wait_ge(xb_ok, 1)
                ins = dve.tensor_tensor(x1[:, t, :], x1[:, t, :], x_sb[:, t, :], ALU.add)
                ins.then_inc(x1_ok, 1)
                dve.wait_ge(x1_ok, c + 1)
                statistics(x1[:, t, :], ts, EPS_PRE)
                normalize(xn2[:, t, :], x1[:, t, :], ts, NORMS + 2 + 2 * c).then_inc(xn2_ok, 1)
                dve.wait_ge(xn2T_hi, c + 1)
                lo_part(xn2T[:, 1, tok], Ob[:, :], xn2T[:, 0, tok]).then_inc(xn2T_lo, 1)
                dve.wait_ge(lg_mm, c + 1)
                dve.tensor_tensor(lg[:], Rb[:, 0:CT * E].rearrange("p (t e) -> p t e", t=CT),
                                  rb_b[:, None, :].to_broadcast([P, CT, E]), ALU.add).then_inc(lg_ok, 1)
                dve.wait_ge(lg_ok, c + 1)
                for i in range(CT):
                    last = dve.max(top[:, i, :], lg[:, i, :])
                link(last)
                dve.tensor_tensor(gd[:], top[:, :, 1], top[:, :, 0], ALU.subtract).then_inc(gap_ok, 1)
                for i in range(CT):
                    last = dve.max_index(topi[:, i, :], top[:, i, :], lg[:, i, :])
                link(last)
                link(dve.tensor_copy(topf[:], topi[:]))
                dve.wait_ge(ge_ok, c + 1)
                link(dve.tensor_scalar(g1[:], ge[:], 1.0, None, ALU.add))
                link(dve.reciprocal(gw0[:], g1[:]))
                link(dve.tensor_tensor(gw1[:], ge[:], gw0[:], ALU.mult))
                for i in range(CT):
                    dve.tensor_scalar(ca[:, i, :], iota8[:], topf[:, i, 0:1], gw0[:, i:i + 1], ALU.is_equal, ALU.mult)
                    last = dve.tensor_scalar(cb[:, i, :], iota8[:], topf[:, i, 1:2], gw1[:, i:i + 1], ALU.is_equal, ALU.mult)
                link(last)
                dve.tensor_tensor(cw[:], ca[:], cb[:], ALU.add).then_inc(cw_ok, 1)
                dve.wait_ge(cwT_mm, c + 1)
                if c:
                    dve.wait_ge(cw_st, 16 * c)
                dve.tensor_copy(cwT[:, :], Ob[0:E, :]).then_inc(cwT_ok, 1)

            tail(0)
            tail(1)

            def hidden(k, i):
                for f in range(FC):
                    slot = (i % 2) * FC + f
                    if f < FC - 1:
                        dve.wait_ge(h_hi, 12 * k + 3 * i + f + 1)
                    else:
                        dve.wait_ge(gelu_done, 16 * k + 4 * i + FC)
                        dve.tensor_copy(Hs[:, 0, slot, :], Hf[:, f, :]).then_inc(h_hi3, 1)
                        dve.wait_ge(h_hi3, 4 * k + i + 1)
                    lo_part(Hs[:, 1, slot, :], Hf[:, f, :], Hs[:, 0, slot, :]).then_inc(h_lo, 1)

            def gather(k, i):
                c = i % CHUNKS
                dve.wait_ge(cwB_ok[i % 2], 32 * k + 16 * (i // 2 + 1))
                dve.wait_ge(w2_done, 4 * k + i + 2)
                dve.wait_ge(y_done, 4 * k + i + 2)
                dve.scalar_tensor_tensor(tmp[:], Yb[c], b2_sb[:, bass.ds(2 * k + i // CHUNKS, 1)], cwB[:, i % 2, :],
                                         ALU.add, ALU.mult).then_inc(y_part, 1)
                dve.wait_ge(y_part, 4 * k + i + 1)
                part = acc[:, c * CH:(c + 1) * CH]
                dve.tensor_tensor(part, part, tmp[:], ALU.add).then_inc(y_done, 1)

            hidden(0, 0)
            dve.wait_ge(acc_zero, 1)
            with dve.Fori(0, E // 2 - 1) as k:
                for i in range(4):
                    hidden(k, i + 1)
                    gather(k, i)
            for i in range(4):
                if i < 3:
                    hidden(E // 2 - 1, i + 1)
                gather(E // 2 - 1, i)

            for c in range(CHUNKS):
                t = slice(c * CT, (c + 1) * CT)
                ts = list(range(c * CT, (c + 1) * CT))
                z = y_att[:, t, :]
                dve.wait_ge(accT_mm, c + 1)
                link(dve.tensor_tensor(z, (Ob, Rb)[c][:, :].rearrange("p (t n) -> p t n", t=CT), xn2[:, t, :], ALU.add))
                statistics(z, ts, EPS_MOE)
                link(normalize(z, z, ts, NORMS + 1 + 2 * CHUNKS + c))
                link(dve.tensor_tensor(z, z, over_rows(l2w), ALU.mult))
                dve.wait_ge(xb_ok, 2)
                dve.tensor_tensor(z, z, x_sb[:, t, :], ALU.add).then_inc(res_ok, 1)


def kernel(**inputs):
    import numpy as np
    import concourse.bacc as bacc
    from concourse.bass_utils import run_bass_kernel_spmd

    a = {k: np.asarray(v) for k, v in inputs.items()}
    wkv = a["L0_xattn_Wkv"]

    def tiles(w):
        return w.reshape(-1, P, w.shape[1]).transpose(1, 0, 2)

    w1, w2 = a["L0_ffn_w1"], a["L0_ffn_w2"]
    laid = {
        "x": a["x"].reshape(TILES, P, DIM).transpose(1, 0, 2),
        "ctx_t": tiles(a["ctx_2048"].reshape(B * M, CTX).T),
        "wq": a["L0_xattn_Wq"],
        "wk": tiles(wkv[:, :INNER]),
        "wv": tiles(wkv[:, INNER:]),
        "wout": tiles(a["L0_xattn_Wout"]),
        "rows": np.concatenate([a["L0_xattn_ln_scale"], a["L0_xattn_ln_bias"], a["L0_ffn_ln_w"], a["L0_ffn_ln_b"],
                                a["L0_ffn_router_b"], a["L0_xattn_null_kv"][0]])[None],
        "columns": np.concatenate([a["L0_ffn_b1"].reshape(E * FC, P).T, a["L0_ffn_b2"].T, a["L0_ffn_router_w"].T,
                                   np.concatenate([a["L0_xattn_null_kv"][1]] * 2)[:, None]], axis=1),
        "w1_t": w1.transpose(0, 2, 1),
        "w2_t": w2.reshape(E, DIM, FC, P).transpose(0, 3, 2, 1).reshape(E, P, FF),
    }
    laid = {k: np.ascontiguousarray(v) for k, v in laid.items()}
    nc = bacc.Bacc("TRN2", target_bir_lowering=False, num_devices=1)
    args = {k: nc.dram_tensor(f"in_{k}", v.shape, mybir.dt.from_np(v.dtype), kind="ExternalInput").ap() for k, v in laid.items()}
    out = nc.dram_tensor("out_0", (P, TILES, DIM), F32, kind="ExternalOutput").ap()
    build(nc, *args.values(), out)
    r = run_bass_kernel_spmd(nc, [{f"in_{k}": v for k, v in laid.items()}], core_ids=[0])
    got = r.results[0]["out_0"]
    return got.transpose(1, 0, 2).reshape(B, N, DIM)
```

```python
import math
from contextlib import ExitStack

import concourse.bass as bass
from concourse import mybir

F32 = mybir.dt.float32
F32R = mybir.dt.float32r
U32 = mybir.dt.uint32
ALU = mybir.AluOpType
ACT = mybir.ActivationFunctionType
AX = mybir.AxisListType

P = 128
B, N, DIM = 4, 256, 128
M, CTX = 256, 256
HEADS, DH = 16, 64
INNER = HEADS * DH
PAIRS = HEADS // 2
UNITS = PAIRS
QT = N // P
KT = M // P
CK = CTX // P
TOK = B * N
TILES = TOK // P
E, FF = 8, 512
FC = FF // P
CH = 512
CHUNKS = TOK // CH
CT = CH // P
VP = 4
SCALE = DH ** -0.5
NORMS = 2
EPS_PRE, EPS_ATT, EPS_MOE = 1e-5, 1e-6, 1e-12
ROWS = 4 * DIM + E + DH
COLS = E * FC + 2 * E + 1
PART = (slice(0, 2 * P), slice(2 * P, INNER))
BOTH = 4
SPLIT = ((0, 0), (0, 1), (1, 0))


def build(nc, x, ctx_t, wq, wk, wv, wout, rows, columns, w1_t, w2_t, out):
    stack = ExitStack()
    with stack:
        def sb(name, shape, dt=F32):
            return stack.enter_context(nc.sbuf_tensor(name, shape, dt))

        def sem(name):
            return stack.enter_context(nc.semaphore(name))

        x_sb = sb("x_sb", [P, TILES, DIM])
        xn = sb("xn", [P, TILES, DIM])
        x1 = xn
        xnT = sb("xnT", [P, 2, TOK], F32R)
        wq_s = sb("wq_s", [P, 2, INNER], F32R)
        wk_s = sb("wk_s", [P, 2, CK, INNER], F32R)
        wv_s = sb("wv_s", [P, 2, CK, INNER], F32R)
        wout_s = sb("wout_s", [P, 2, PAIRS, DIM], F32R)
        ctxT = sb("ctxT", [P, 2, CK, TOK], F32R)
        ctxV = sb("ctxV", [P, 2, CK, M], F32R)
        QK = sb("QK", [P, 2, UNITS, N + M], F32R)
        Hs = QK
        V = sb("V", [P, KT, INNER])
        Hf = V[:, :, :].rearrange("p k (f n) -> p (k f) n", n=CH)
        wq_raw = V[:, 0, :]
        Pr = sb("Pr", [P, 2, 2, QT, M])
        cwB = Pr[:, 0, :, :, :].rearrange("p h t m -> p (h t m)").rearrange("p (s n) -> p s n", s=2)
        PT = sb("PT", [P, 2, 2, KT * N])
        wk_raw = PT[:, :, :, :].rearrange("p a h n -> p (a h n)").rearrange("p (k n) -> p k n", k=CK)
        O = sb("O", [P, 2, UNITS, N], F32R)
        y_att = sb("y_att", [P, TILES, DIM])
        yT = sb("yT", [P, TOK])
        xn2 = sb("xn2", [P, TILES, DIM])
        ctx_raw = [yT[:, :], xn2[:, :, :].rearrange("p t n -> p (t n)")]
        xn2T = sb("xn2T", [P, 2, TOK], F32R)
        Wraw = sb("Wraw", [P, 2, 2, FF])
        wv_raw = Wraw[:, :, :, :].rearrange("p s w n -> p (s w n)").rearrange("p (k n) -> p k n", k=CK)
        Ws = wk_s
        acc = sb("acc", [P, TOK])
        wout_raw = acc[:, :].rearrange("p (c n) -> p c n", c=PAIRS)
        tmp = sb("tmp", [P, CH])
        ident = sb("ident", [P, P])
        rows_b = sb("rows_b", [P, ROWS])
        l1w, l1b, l2w, l2b = (rows_b[:, i * DIM:(i + 1) * DIM] for i in range(4))
        rb_b, nk_b = rows_b[:, 4 * DIM:4 * DIM + E], rows_b[:, 4 * DIM + E:ROWS]
        cols_sb = sb("cols_sb", [P, COLS])
        b1_sb, b2_sb, rw_f, nv_col = (cols_sb[:, a:b] for a, b in ((0, E * FC), (E * FC, E * FC + E),
                                                                   (E * FC + E, E * FC + 2 * E), (COLS - 1, COLS)))
        NVB = sb("NVB", [P, PAIRS, HEADS])
        NKf = sb("NKf", [P, HEADS])
        NK_s = sb("NK_s", [P, 2, HEADS], F32R)
        NW = sb("NW", [HEADS, DIM])
        nsn = sb("nsn", [P, TILES, HEADS])
        pn = sb("pn", [P, TILES, HEADS])
        pnT = sb("pnT", [HEADS, CH])
        mx = sb("mx", [P, 4, 4])
        nm = sb("nm", [P, 4, 4])
        t4 = sb("t4", [P, 4, 4])
        en = sb("en", [P, 4, 4])
        sm = sb("sm", [P, 4, 4])
        den = sb("den", [P, 4, 4])
        rden = sb("rden", [P, 4, 4])
        st = sb("st", [P, TILES, 6])
        mv = sb("mv", [P, TILES, 2])
        ve = sb("ve", [P, TILES])
        rstd = sb("rstd", [P, TILES])
        mhalf = sb("mhalf", [P, TILES])
        spare = sb("spare", [P, 1])
        euler = sb("euler", [P, CT])
        iota8 = sb("iota8", [P, E])
        rw_s = sb("rw_s", [P, 2, E], F32R)
        lg = sb("lg", [P, CT, E])
        top = sb("top", [P, CT, E])
        topi = sb("topi", [P, CT, E], U32)
        topf = sb("topf", [P, CT, E])
        gd = sb("gd", [P, CT])
        ge = sb("ge", [P, CT])
        g1 = sb("g1", [P, CT])
        gw0 = sb("gw0", [P, CT])
        gw1 = sb("gw1", [P, CT])
        ca = sb("ca", [P, CT, E])
        cb = sb("cb", [P, CT, E])
        cw = sb("cw", [P, CT, E])
        cwT = sb("cwT", [E, CH])
        cw_dram = nc.dram_tensor("cw_scratch", (E, TOK), F32, kind="Internal").ap()

        S = stack.enter_context(nc.psum_tensor("S", [P, 2, 2, QT * M], F32))
        Tb = stack.enter_context(nc.psum_tensor("Tb", [P, 2, KT * N], F32))
        Ob = stack.enter_context(nc.psum_tensor("Ob", [P, 512], F32))
        Rb = stack.enter_context(nc.psum_tensor("Rb", [P, 512], F32))
        lead_banks = [(Tb[:, 0, :], Tb[:, 1, :], Ob[:, :])[c % 3] for c in range(UNITS)]
        XPARTS = [((0, 1), S[:, 1, 1, 0:N]), ((1, 3), Rb[:, :]), ((3, 4), Ob[:, 0:N])]
        Hb = [S[:, 0, 0, :], S[:, 0, 1, :], S[:, 1, 0, :], S[:, 1, 1, :]]
        Yb = [Tb[:, 0, :], Tb[:, 1, :]]

        ld_x0, ld_x, ld_ctx0, ld_ctx1, ld_wout, ld_small = (
            sem(n) for n in ("ld_x0", "ld_x", "ld_ctx0", "ld_ctx1", "ld_wout", "ld_small"))
        ld_wq, ld_wk, ld_wv = ([sem(f"ld_{n}{h}") for h in range(2)] for n in ("wq", "wk", "wv"))
        ident_ok, const_ok = sem("ident_ok"), sem("const_ok")
        var_ok, rstd_ok, xn_ok = sem("var_ok"), sem("rstd_ok"), sem("xn_ok")
        xnT_mm, xnT_hi, xnT_lo = sem("xnT_mm"), sem("xnT_hi"), sem("xnT_lo")
        wq_hi, wq_lo, wk_hi, wk_lo, wv_hi, wv_lo = (sem(n) for n in ("wq_hi", "wq_lo", "wk_hi", "wk_lo", "wv_hi", "wv_lo"))
        ctx0_hi, ctx0_lo, ctx1_hi, ctx1_lo, wout_hi, wout_lo, ctxV_ok = (
            sem(n) for n in ("ctx0_hi", "ctx0_lo", "ctx1_hi", "ctx1_lo", "wout_hi", "wout_lo", "ctxV_ok"))
        nk_prod, nk_lo, ns_mm, ns_ok = (sem(n) for n in ("nk_prod", "nk_lo", "ns_mm", "ns_ok"))
        qk_mm, qk_hi, qk_lo = sem("qk_mm"), sem("qk_hi"), sem("qk_lo")
        v_mm, v_sb = sem("v_mm"), sem("v_sb")
        s_done, mx_ok, nm_ok, t4_ok, exp_done = (sem(n) for n in ("s_done", "mx_ok", "nm_ok", "t4_ok", "exp_done"))
        den_ok, rden_ok, pn_ok, scaled = (sem(n) for n in ("den_ok", "rden_ok", "pn_ok", "scaled"))
        t_done, pt_sb, pt_sb2, pv_done, o_hi, o_lo = (sem(n) for n in ("t_done", "pt_sb", "pt_sb2", "pv_done", "o_hi", "o_lo"))
        out_mm, y_sb = sem("out_mm"), sem("y_sb")
        nvb_ok, nw_mm, nw_sb, pnT_mm, pnT_sb, x1_ok, xn2_ok, xn2T_mm, xn2T_hi, xn2T_lo, y_mm = (
            sem(n) for n in ("nvb_ok", "nw_mm", "nw_sb", "pnT_mm", "pnT_sb", "x1_ok", "xn2_ok", "xn2T_mm", "xn2T_hi", "xn2T_lo", "y_mm"))
        rw_lo, lg_mm, lg_ok, gap_ok, ge_ok, cw_ok, cwT_mm, cwT_ok, accT_mm, res_ok, dve_link, h_hi3 = (
            sem(n) for n in ("rw_lo", "lg_mm", "lg_ok", "gap_ok", "ge_ok", "cw_ok", "cwT_mm", "cwT_ok", "accT_mm", "res_ok", "dve_link", "h_hi3"))
        acc_ok, xb_ok = sem("acc_ok"), sem("xb_ok")
        cw_st, cwB_ok = sem("cw_st"), [sem("cwB_ok0"), sem("cwB_ok1")]
        wraw_ok, wsplit = [sem("wraw_ok0"), sem("wraw_ok1")], sem("wsplit")
        w1_done, gelu_done, h_hi, h_lo, w2_done, y_part, y_done = (
            sem(n) for n in ("w1_done", "gelu_done", "h_hi", "h_lo", "w2_done", "y_part", "y_done"))
        store = sem("store")
        pool_past, act_past = sem("pool_past"), sem("act_past")

        def place(k, i):
            return (i % 2, i // 2) if isinstance(k, int) and k == 0 else (i // CHUNKS, i % CHUNKS)

        block = stack.enter_context(nc.Block())

        @block.sync
        def _(sp):
            sp.dma_start(x_sb[:, 0:QT, :], x[:, 0:QT, :]).then_inc(ld_x0, 16)
            half = [slice(h * INNER // 2, (h + 1) * INNER // 2) for h in range(2)]
            sp.dma_start(wq_raw[:, PART[0]], wq[:, PART[0]]).then_inc(ld_wq[0], 16)
            for k in range(CK):
                sp.dma_start(ctx_raw[k][:, 0:M], ctx_t[:, k, 0:M]).then_inc(ld_ctx0, 16)
            sp.dma_start(wk_raw[:, :, PART[0]], wk[:, :, PART[0]]).then_inc(ld_wk[0], 16)
            sp.dma_start(wq_raw[:, PART[1]], wq[:, PART[1]]).then_inc(ld_wq[1], 16)
            sp.dma_start(wk_raw[:, :, PART[1]], wk[:, :, PART[1]]).then_inc(ld_wk[1], 16)
            sp.dma_start(x_sb[:, QT:TILES, :], x[:, QT:TILES, :]).then_inc(ld_x, 16)
            sp.dma_start(wv_raw[:, :, half[0]], wv[:, :, half[0]]).then_inc(ld_wv[0], 16)
            for k in range(CK):
                sp.dma_start(ctx_raw[k][:, M:TOK], ctx_t[:, k, M:TOK]).then_inc(ld_ctx1, 16)
            sp.dma_start(wv_raw[:, :, half[1]], wv[:, :, half[1]]).then_inc(ld_wv[1], 16)
            sp.dma_start(wout_raw, wout).then_inc(ld_wout, 16)

            def load_expert(e, s):
                sp.dma_start(Wraw[:, s, 0, :], w1_t[bass.ds(e, 1), :, :].rearrange("e p n -> p (e n)")).then_inc(wraw_ok[s], 16)
                sp.dma_start(Wraw[:, s, 1, :], w2_t[bass.ds(e, 1), :, :].rearrange("e p n -> p (e n)")).then_inc(wraw_ok[s], 16)

            def gate(e, c, s):
                sp.dma_start(cwB[:, s, :], cw_dram[bass.ds(e, 1), c * CH:(c + 1) * CH].to_broadcast([P, CH])).then_inc(cwB_ok[s], 16)

            sp.wait_ge(wv_hi, 2)
            sp.wait_ge(wv_lo, 2)
            load_expert(0, 0)
            load_expert(1, 1)
            def store_gates(c):
                sp.wait_ge(cwT_ok, c + 1)
                sp.dma_start(cw_dram[:, c * CH:(c + 1) * CH], cwT[:, :]).then_inc(cw_st, 16)
                sp.wait_ge(cw_st, 16 * (c + 1))

            def gates(k, i):
                e, c = place(k, i)
                if not (isinstance(k, int) and k == 0 and i < 2):
                    sp.wait_ge(y_done, 4 * k + i + 1)
                gate(2 * k + e, c, i % 2)

            for e in range(2, 4):
                sp.wait_ge(wsplit, 4 * (e - 1))
                load_expert(e, e % 2)
            store_gates(0)
            gates(0, 0)
            gates(0, 1)
            store_gates(1)
            gates(0, 2)
            gates(0, 3)
            with sp.Fori(1, E // 2 - 1) as k:
                for s in range(2):
                    sp.wait_ge(wsplit, 4 * (2 * k + s + 1))
                    load_expert(2 * k + s + 2, s)
                    gates(k, 2 * s)
                    gates(k, 2 * s + 1)
            for i in range(4):
                gates(E // 2 - 1, i)
            for c in range(CHUNKS):
                sp.wait_ge(res_ok, c + 1)
                sp.dma_start(out[:, c * CT:(c + 1) * CT, :], y_att[:, c * CT:(c + 1) * CT, :]).then_inc(store, 16)
            sp.wait_ge(store, 16 * CHUNKS)

        @block.gpsimd
        def _(pool):
            pool.memset(ident[:], 0.0).then_inc(ident_ok, 1)
            pool.wait_ge(ident_ok, 1)
            pool.affine_select(out=ident[:], in_=ident[:], compare_op=ALU.not_equal, fill=1.0, base=0,
                               pattern=[[-1, P]], channel_multiplier=1).then_inc(ident_ok, 1)
            pool.memset(mhalf[:], -0.5).then_inc(const_ok, 1)
            pool.memset(euler[:], math.e).then_inc(const_ok, 1)
            pool.iota(iota8[:], pattern=[[1, E]], base=0, channel_multiplier=0,
                      allow_small_or_imprecise_dtypes=True).then_inc(const_ok, 1)
            pool.memset(NVB[:], 0.0).then_inc(const_ok, 1)
            pool.wait_ge(const_ok, 1)
            pool.wait_ge(var_ok, 1)
            pool.tensor_tensor(rstd[:, 0:QT], ve[:, 0:QT], mhalf[:, 0:QT], ALU.pow).then_inc(rstd_ok, 1)
            for h in range(2):
                pool.wait_ge(ld_wq[h], 16)
            pool.wait_ge(ld_small, 32)
            pool.tensor_tensor(y_att[:, :, :].rearrange("p t n -> p (t n)").rearrange("p (h d) -> p h d", d=DH),
                               wq_raw.rearrange("p (h d) -> p h d", d=DH),
                               nk_b[:, None, :].to_broadcast([P, HEADS, DH]), ALU.mult).then_inc(nk_prod, 1)
            pool.wait_ge(ctx0_lo, CK)
            for r in range(2):
                pool.tensor_copy(ctxV[:, r, :, :], ctxT[:, r, :, 0:M]).then_inc(ctxV_ok, 1)

            def wv_part(h):
                cols = slice(h * INNER // 2, (h + 1) * INNER // 2)
                pool.wait_ge(wv_hi, h + 1)
                pool.tensor_tensor(wv_s[:, 1, :, cols], wv_raw[:, :, cols], wv_s[:, 0, :, cols].bitcast(F32),
                                   ALU.subtract).then_inc(wv_lo, 1)

            def scale(b, p):
                pool.wait_ge(rden_ok, UNITS * b + p + 1)
                pool.sem_inc(pool_past, 1)
                for h in range(2):
                    for q in range(QT):
                        last = pool.tensor_scalar(Pr[:, p % 2, h, q, :], Pr[:, p % 2, h, q, :],
                                                  rden[:, p % 4, h * QT + q:h * QT + q + 1], 1.0, ALU.mult, ALU.mult)
                last.then_inc(scaled, 1)

            def ctx_part(k):
                pool.wait_ge(ctx1_hi, k + 1)
                pool.tensor_tensor(ctxT[:, 1, k, M:TOK], ctx_raw[k][:, M:TOK], ctxT[:, 0, k, M:TOK].bitcast(F32),
                                   ALU.subtract).then_inc(ctx1_lo, 1)

            wv_part(0)
            ctx_part(0)
            pool.wait_ge(var_ok, 2)
            pool.tensor_tensor(rstd[:, QT:TILES], ve[:, QT:TILES], mhalf[:, QT:TILES], ALU.pow).then_inc(rstd_ok, 1)
            ctx_part(1)
            scale(0, 0)
            wv_part(1)
            scale(0, 1)
            scale(0, 2)
            pool.wait_ge(wout_hi, 1)
            pool.tensor_tensor(wout_s[:, 1, :, :], wout_raw, wout_s[:, 0, :, :].bitcast(F32), ALU.subtract).then_inc(wout_lo, 1)

            pool.tensor_tensor(x_sb[:], x_sb[:], l1b[:, None, :].to_broadcast([P, TILES, DIM]), ALU.add).then_inc(xb_ok, 1)

            def split(e, s, ws=(0, 1)):
                for w in ws:
                    hi, lo = (Ws[:, r, s, w * FF:(w + 1) * FF] for r in range(2))
                    pool.tensor_scalar(hi, Wraw[:, s, w, :], 1.0, 1.0, ALU.mult, ALU.mult).then_inc(wsplit, 1)
                    pool.wait_ge(wsplit, 4 * e + 2 * w + 1)
                    pool.tensor_tensor(lo, Wraw[:, s, w, :], hi.bitcast(F32), ALU.subtract).then_inc(wsplit, 1)

            def power(c, n):
                t = slice(c * CT, (c + 1) * CT)
                count = NORMS + 2 * c + n + 1 if n < 2 else NORMS + 2 * CHUNKS + c + 1
                pool.wait_ge(var_ok, count)
                pool.tensor_tensor(rstd[:, t], ve[:, t], mhalf[:, t], ALU.pow).then_inc(rstd_ok, 1)

            def gap(c):
                pool.wait_ge(gap_ok, c + 1)
                pool.tensor_tensor(ge[:], euler[:], gd[:], ALU.pow).then_inc(ge_ok, 1)

            def body(b, last):
                for p in range(1, UNITS):
                    if p + 2 < UNITS:
                        scale(b, p + 2)
                    elif not last:
                        scale(b + 1, p + 2 - UNITS)
                    if p in (2, 3) and not last:
                        if p == 2:
                            pool.wait_ge(v_mm, VP * (b + 1))
                            pool.sem_inc(pool_past, 1)
                        pool.tensor_copy(ctxV[:, p - 2, :, :],
                                         ctxT[:, p - 2, :, bass.ds((b + 1) * M, M)]).then_inc(ctxV_ok, 1)
                    if last and p in (3, 5):
                        power(0, (p - 3) // 2)
                    if last and p in (1, 2, 6):
                        if p == 1:
                            pool.wait_ge(qk_mm, UNITS * B)
                        if p in (1, 6):
                            pool.wait_ge(wraw_ok[p // 6], 32)
                        split(p // 6, p // 6, {1: (0,), 2: (1,), 6: (0, 1)}[p])
                if not last:
                    scale(b + 1, 2)

            with pool.Fori(0, B - 1) as b:
                body(b, False)
            body(B - 1, True)

            gap(0)
            power(1, 0)
            power(1, 1)
            gap(1)
            for e in range(2, 4):
                pool.wait_ge(w2_done, e + 2)
                pool.wait_ge(wraw_ok[e % 2], 64)
                split(e, e % 2)
            pool.wait_ge(x1_ok, CHUNKS)
            pool.wait_ge(xn2_ok, CHUNKS)
            pool.tensor_tensor(x_sb[:], x1[:], l2b[:, None, :].to_broadcast([P, TILES, DIM]), ALU.add).then_inc(xb_ok, 1)
            with pool.Fori(2, E // 2) as k:
                for s in range(2):
                    pool.wait_ge(w2_done, 4 * k + 2 * s - 1)
                    pool.wait_ge(wraw_ok[s], 32 * (k + 1))
                    pool.sem_inc(pool_past, 1)
                    split(2 * k + s, s)
            for c in range(CHUNKS):
                power(c, 2)

        @block.scalar
        def _(act):
            act.dma_start(rows_b[:], rows.to_broadcast([P, ROWS])).then_inc(ld_small, 16)
            act.dma_start(cols_sb[:], columns).then_inc(ld_small, 16)
            half = [slice(h * INNER // 2, (h + 1) * INNER // 2) for h in range(2)]

            def hi_part(dst, full, done):
                act.activation(dst, full, ACT.Copy).then_inc(done, 1)

            def ctx_part(loaded, cols, done):
                act.wait_ge(loaded, 16 * CK)
                for k in range(CK):
                    hi_part(ctxT[:, 0, k, cols], ctx_raw[k][:, cols], done)

            def wq_part(h):
                act.wait_ge(ld_wq[h], 16)
                hi_part(wq_s[:, 0, PART[h]], wq_raw[:, PART[h]], wq_hi)

            def wk_part(h):
                act.wait_ge(ld_wk[h], 16)
                hi_part(wk_s[:, 0, :, PART[h]], wk_raw[:, :, PART[h]], wk_hi)

            def wv_part(h):
                act.wait_ge(ld_wv[h], 16)
                hi_part(wv_s[:, 0, :, half[h]], wv_raw[:, :, half[h]], wv_hi)

            def xnT_part(i):
                (g0, g1), bank = XPARTS[i]
                act.wait_ge(xnT_mm, i + 1)
                hi_part(xnT[:, 0, g0 * N:g1 * N], bank, xnT_hi)

            def qk_part(b, c, bank):
                act.wait_ge(qk_mm, UNITS * b + c + 1)
                act.activation(QK[:, 0, c, :], bank, ACT.Copy).then_inc(qk_hi, 1)

            def exps(b, p, u):
                act.wait_ge(t4_ok, UNITS * b + p + 1)
                act.activation(en[:, p % 4, :], t4[:, p % 4, :], ACT.Exp)
                if not (isinstance(u, int) and u < 2):
                    act.wait_ge(t_done, UNITS * b + p - 1)
                for h in range(2):
                    for q in range(QT):
                        i = h * QT + q
                        last = act.activation(Pr[:, p % 2, h, q, :], S[:, p % 2, h, q * M:(q + 1) * M], ACT.Exp,
                                              bias=nm[:, p % 4, i:i + 1], scale=SCALE,
                                              accum_out=sm[:, p % 4, i:i + 1])
                last.then_inc(exp_done, 1)

            def values(b, i, bank):
                half, kt = i // 2, i % 2
                act.wait_ge(v_mm, VP * b + i + 1)
                act.activation(V[:, kt, half * 512:(half + 1) * 512], bank, ACT.Copy).then_inc(v_sb, 1)

            def probabilities(b, p, both=False):
                act.wait_ge(t_done, UNITS * b + p + 1)
                if both:
                    act.activation(PT[:, p % 2, 0, :], Tb[:, 0, :], ACT.Copy).then_inc(pt_sb, 1)
                act.activation(PT[:, p % 2, 1, :], Tb[:, 1, :], ACT.Copy).then_inc(pt_sb2, 1)

            def o_part(b, p):
                act.wait_ge(pv_done, UNITS * b + p + 1)
                act.activation(O[:, 0, p, :], Ob[:, 0:N], ACT.Copy).then_inc(o_hi, 1)

            wq_part(0)
            ctx_part(ld_ctx0, slice(0, M), ctx0_hi)
            xnT_part(0)
            wk_part(0)
            wq_part(1)
            qk_part(0, 0, lead_banks[0])
            wk_part(1)
            qk_part(0, 1, lead_banks[1])
            wv_part(0)
            ctx_part(ld_ctx1, slice(M, TOK), ctx1_hi)
            qk_part(0, 2, lead_banks[2])
            qk_part(0, 3, lead_banks[3])
            exps(0, 0, 0)
            qk_part(0, 4, lead_banks[4])
            qk_part(0, 5, lead_banks[5])
            wv_part(1)
            exps(0, 1, 1)
            qk_part(0, 6, lead_banks[6])
            xnT_part(1)
            qk_part(0, 7, lead_banks[7])
            xnT_part(2)
            act.wait_ge(wq_lo, 2)
            act.wait_ge(nk_prod, 1)
            values(0, 0, Rb[:, :])
            values(0, 1, Ob[:, :])
            act.wait_ge(ld_wout, 16)
            hi_part(wout_s[:, 0, :, :], wout_raw, wout_hi)
            probabilities(0, 0)
            exps(0, 2, 2)
            probabilities(0, 1)

            def input_transposed(c, bank):
                act.wait_ge(xn2T_mm, c + 1)
                act.activation(xn2T[:, 0, c * CH:(c + 1) * CH], bank[:, :], ACT.Copy).then_inc(xn2T_hi, 1)
                act.wait_ge(wout_lo, 1)
                act.wait_ge(nw_mm, 1)
                act.activation(acc[:, c * CH:(c + 1) * CH], bank[:, :], ACT.Copy).then_inc(acc_ok, 1)

            def body(b, last):
                def next_probabilities(p):
                    if p + 1 < UNITS:
                        probabilities(b, p + 1, last and p + 1 >= BOTH)
                    elif not last:
                        probabilities(b + 1, 0)

                for p in range(1, UNITS):
                    with_values = p in (1, 2) or p in (5, 6) and not last
                    o_part(b, p - 1)
                    if p + 2 < UNITS:
                        exps(b, p + 2, None)
                    elif not last:
                        exps(b + 1, p + 2 - UNITS, None)
                    if with_values:
                        if p in (1, 2):
                            values(b, p + 1, Rb[:, :])
                        else:
                            values(b + 1, p - 5, Rb[:, :])
                        next_probabilities(p)
                    if last and p == 6:
                        act.activation(spare[:], mhalf[:, 0:1], ACT.Gelu)
                    if last and p == 7:
                        input_transposed(0, Rb)
                    if not last:
                        qk_part(b + 1, p - 1, Rb[:, :])
                    if not with_values:
                        next_probabilities(p)
                o_part(b, UNITS - 1)
                if not last:
                    exps(b + 1, 2, None)
                    probabilities(b + 1, 1)
                act.wait_ge(out_mm, b + 1)
                act.sem_inc(act_past, 1)
                act.activation(yT[:, bass.ds(N * b, N)], (S[:, 0, 1, :] if last else Rb)[:, 0:N], ACT.Copy).then_inc(y_sb, 1)
                if not last:
                    qk_part(b + 1, UNITS - 1, Rb[:, :])

            with act.Fori(0, B - 1) as b:
                body(b, False)
            body(B - 1, True)

            def gelus(k, i):
                for f in range(FC):
                    act.wait_ge(w1_done, 16 * k + 4 * i + f + 1)
                    if not (isinstance(k, int) and 4 * k + i == 0):
                        act.wait_ge(h_lo, 16 * k + 4 * (i - 1) + f + 1)
                    act.sem_inc(act_past, 1)
                    act.activation(Hf[:, f, :], Hb[f], ACT.Gelu,
                                   bias=b1_sb[:, bass.ds(2 * FC * k + place(k, i)[0] * FC + f, 1)]).then_inc(gelu_done, 1)
                    if f < FC - 1:
                        if f == 0 and not (isinstance(k, int) and 4 * k + i == 0):
                            act.wait_ge(w2_done, 4 * k + i)
                        act.wait_ge(gelu_done, 16 * k + 4 * i + f + 1)
                        act.activation(Hs[:, 0, (i % 2) * FC + f, :], Hf[:, f, :], ACT.Copy).then_inc(h_hi, 1)

            gelus(0, 0)
            input_transposed(1, Rb)
            gelus(0, 1)
            gelus(0, 2)
            gelus(0, 3)
            gelus(1, 0)
            with act.Fori(1, E // 2 - 1) as k:
                for i in range(1, 5):
                    gelus(k, i)
            for i in range(1, 4):
                gelus(E // 2 - 1, i)

        @block.tensor
        def _(pe):
            pe.sem_inc(w2_done, 1)

            def products(dst, left, right):
                steps = [(a[0 + x_], b_[0 + y_]) for a, b_ in zip(left, right) for x_, y_ in SPLIT]
                for n, (a, b_) in enumerate(steps):
                    last = pe.matmul(dst, a, b_, start=n == 0, stop=n == len(steps) - 1)
                return last

            def qk(b, c, bank):
                cols = slice(c * P, (c + 1) * P)
                products(bank[:, 0:N], [[wq_s[:, r, cols] for r in range(2)]],
                         [[xnT[:, r, bass.ds(b * N, N)] for r in range(2)]])
                products(bank[:, N:N + M], [[wk_s[:, r, k, cols] for r in range(2)] for k in range(CK)],
                         [[ctxT[:, r, k, bass.ds(b * M, M)] for r in range(2)] for k in range(CK)]).then_inc(qk_mm, 1)

            def value(b, i, bank):
                half, kt = i // 2, i % 2
                if i == 0:
                    pe.wait_ge(ctxV_ok, 2 * (b + 1))
                products(bank, [[ctxV[:, r, k, kt * P:(kt + 1) * P] for r in range(2)] for k in range(CK)],
                         [[wv_s[:, r, k, half * 512:(half + 1) * 512] for r in range(2)] for k in range(CK)]).then_inc(v_mm, 1)

            def scores(b, p, u):
                pe.wait_ge(qk_lo, UNITS * b + p + 1)
                if not (isinstance(u, int) and u < 2):
                    pe.wait_ge(exp_done, UNITS * b + p - 1)
                for q in range(QT):
                    for n, (i, j) in enumerate(SPLIT):
                        for h in range(2):
                            rows = slice(h * DH, (h + 1) * DH)
                            last = pe.matmul(S[:, p % 2, h, q * M:(q + 1) * M], QK[rows, i, p, q * P:(q + 1) * P],
                                             QK[rows, j, p, N:N + M], start=n == 0, stop=n == len(SPLIT) - 1)
                last.then_inc(s_done, 1)

            def transposes(b, p, u):
                pe.wait_ge(scaled, UNITS * b + p + 1)
                if not (isinstance(u, int) and u < 1):
                    pe.wait_ge(pt_sb, UNITS * b + p)
                    pe.wait_ge(pt_sb2, UNITS * b + p)
                for h in range(2):
                    for q in range(QT):
                        for k in range(KT):
                            last = pe.transpose(Tb[:, h, k * N + q * P:k * N + (q + 1) * P],
                                                Pr[:, p % 2, h, q, k * P:(k + 1) * P], ident[:, :])
                last.then_inc(t_done, 1)

            def attend(b, p):
                pe.wait_ge(pt_sb, UNITS * b + p + 1)
                pe.wait_ge(pt_sb2, UNITS * b + p + 1)
                pe.wait_ge(v_sb, VP * b + (2 if p < UNITS // 2 else 4))
                pe.wait_ge(o_lo, UNITS * b + p + 1)
                for k in range(KT):
                    for h in range(2):
                        head = 2 * p + h
                        last = pe.matmul(Ob[h * DH:(h + 1) * DH, 0:N], V[:, k, head * DH:(head + 1) * DH],
                                         PT[:, p % 2, h, k * N:(k + 1) * N], start=k == 0, stop=k == KT - 1)
                last.then_inc(pv_done, 1)

            def x_transposed(i):
                (g0, g1), bank = XPARTS[i]
                for t in range(QT * g0, QT * g1):
                    pe.wait_ge(xn_ok, t + 1)
                    last = pe.transpose(bank[:, (t - QT * g0) * P:(t - QT * g0 + 1) * P], xn[:, t, :], ident[:, :])
                last.then_inc(xnT_mm, 1)

            def null_keys(ts):
                for t in ts:
                    last = products(Rb[:, t * HEADS:(t + 1) * HEADS],
                                    [[xnT[:, r, t * P:(t + 1) * P] for r in range(2)]], [[NK_s[:, r, :] for r in range(2)]])
                last.then_inc(ns_mm, 1)

            def keep_busy(n):
                for _ in range(n):
                    pe.matmul(Rb[:, 0:P], ident[:, :], ident[:, :], start=True, stop=True)

            pe.wait_ge(ident_ok, 2)
            keep_busy(10)
            x_transposed(0)
            keep_busy(6)
            pe.wait_ge(wq_lo, 1)
            pe.wait_ge(xnT_lo, 1)
            pe.wait_ge(ctx0_lo, CK)
            pe.wait_ge(wk_lo, 1)
            for c in range(2):
                qk(0, c, lead_banks[c])
            scores(0, 0, 0)
            pe.wait_ge(nk_lo, 1)
            null_keys(range(QT))
            pe.wait_ge(wq_lo, 2)
            pe.wait_ge(wk_lo, 2)
            qk(0, 2, lead_banks[2])
            qk(0, 3, lead_banks[3])
            scores(0, 1, 1)
            qk(0, 4, lead_banks[4])
            pe.wait_ge(qk_lo, 3)
            qk(0, 5, lead_banks[5])
            pe.wait_ge(ns_ok, 1)
            pe.wait_ge(nvb_ok, 2)
            pe.wait_ge(ld_wout, 16)
            for c in range(PAIRS):
                last_mm = pe.matmul(Rb[0:HEADS, 0:DIM], NVB[:, c, :], wout_raw[:, c, :], start=c == 0, stop=c == PAIRS - 1)
            last_mm.then_inc(nw_mm, 1)
            pe.wait_ge(qk_lo, 4)
            qk(0, 6, lead_banks[6])
            pe.wait_ge(nw_sb, 1)
            x_transposed(1)
            pe.wait_ge(qk_lo, 5)
            qk(0, 7, lead_banks[7])
            pe.wait_ge(qk_lo, 6)
            x_transposed(2)
            scores(0, 2, 2)
            pe.wait_ge(wv_lo, 1)
            pe.wait_ge(xnT_lo, 2)
            value(0, 0, Rb[:, :])
            pe.wait_ge(xnT_lo, 3)
            value(0, 1, Ob[:, :])
            pe.wait_ge(qk_lo, UNITS)
            transposes(0, 0, 0)
            pe.wait_ge(v_sb, 1)
            null_keys(range(QT, 4))
            scores(0, 3, None)
            null_keys(range(4, 6))
            transposes(0, 1, None)
            null_keys(range(6, TILES))
            attend(0, 0)
            pe.wait_ge(wv_lo, 2)

            def project(b, bank):
                pe.wait_ge(o_lo, UNITS * (b + 1) + 1)
                pe.wait_ge(wout_lo, 1)
                products(bank[:, 0:N], [[wout_s[:, r, c, :] for r in range(2)] for c in range(PAIRS)],
                         [[O[:, r, c, :] for r in range(2)] for c in range(PAIRS)]).then_inc(out_mm, 1)

            def null_transposed(c, bank):
                pe.wait_ge(pn_ok, UNITS * B // CHUNKS * (c + 1))
                for t in range(CT):
                    last = pe.transpose(bank[0:HEADS, t * P:(t + 1) * P], pn[:, c * CT + t, :], ident[:, :])
                last.then_inc(pnT_mm, 1)

            def outputs(c):
                pe.wait_ge(pnT_sb, c + 1)
                for t in range(CT):
                    if t % QT == 0:
                        pe.wait_ge(y_sb, (c * CT + t) // QT + 1)
                    dst = Rb[:, t * DIM:(t + 1) * DIM]
                    pe.matmul(dst, yT[:, (c * CT + t) * P:(c * CT + t + 1) * P], ident[:, :], start=True, stop=False)
                    last = pe.matmul(dst, pnT[:, t * P:(t + 1) * P], NW[:, :], start=False, stop=True)
                last.then_inc(y_mm, 1)

            def input_transposed(c, bank):
                pe.wait_ge(xn2_ok, c + 1)
                for t in range(CT):
                    last = pe.transpose(bank[:, t * P:(t + 1) * P], xn2[:, c * CT + t, :], ident[:, :])
                last.then_inc(xn2T_mm, 1)

            def logits(c):
                if c == 0:
                    pe.wait_ge(o_lo, UNITS * B + 1)
                pe.wait_ge(xn2T_lo, c + 1)
                for t in range(CT):
                    tok = slice((c * CT + t) * P, (c * CT + t + 1) * P)
                    last = products(Ob[:, t * E:(t + 1) * E], [[xn2T[:, r, tok] for r in range(2)]],
                                    [[rw_s[:, r, :] for r in range(2)]])
                last.then_inc(lg_mm, 1)

            def gates_transposed(c):
                pe.wait_ge(cw_ok, c + 1)
                for t in range(CT):
                    last = pe.transpose(Ob[0:E, t * P:(t + 1) * P], cw[:, t, :], ident[:, :])
                last.then_inc(cwT_mm, 1)

            def body(b, last):
                def next_transposes(p):
                    if p + 1 < UNITS:
                        transposes(b, p + 1, None)
                    elif not last:
                        transposes(b + 1, 0, None)

                for p in range(1, UNITS):
                    with_values = p in (1, 2) or p in (5, 6) and not last
                    if last and p == 7:
                        input_transposed(0, Rb)
                    if p + 3 < UNITS:
                        scores(b, p + 3, None)
                    elif not last:
                        scores(b + 1, p + 3 - UNITS, None)
                    if with_values:
                        if last and p == 2:
                            pe.wait_ge(pnT_sb, 1)
                        else:
                            pe.wait_ge(qk_lo, UNITS * (b + 1) + p - 1)
                        if p == 1:
                            pe.wait_ge(ctx1_lo, CK)
                            pe.wait_ge(ns_ok, 2)
                        if p in (1, 2):
                            value(b, p + 1, Rb[:, :])
                        else:
                            value(b + 1, p - 5, Rb[:, :])
                        next_transposes(p)
                        pe.wait_ge(v_sb, VP * b + (p + 2 if p in (1, 2) else p))
                    elif not last:
                        pe.wait_ge(qk_lo, UNITS * (b + 1) + p - 1)
                    if not last:
                        qk(b + 1, p - 1, Rb)
                    elif p == 1:
                        null_transposed(0, Rb)
                    elif p == 2:
                        outputs(0)
                    if not with_values:
                        next_transposes(p)
                    attend(b, p)
                    if last and p == 7:
                        null_transposed(1, S[:, 0, 0, :])
                if not last:
                    scores(b + 1, 3, None)
                    transposes(b + 1, 1, None)
                    pe.wait_ge(qk_lo, UNITS * (b + 2) - 1)
                if last:
                    logits(0)
                project(b, S[:, 0, 1, :] if last else Rb)
                if not last:
                    attend(b + 1, 0)
                    pe.wait_ge(y_sb, b + 1)
                    qk(b + 1, UNITS - 1, Rb)

            with pe.Fori(0, B - 1) as b:
                body(b, False)
            body(B - 1, True)

            def up(k, i):
                e, c = place(k, i)
                s = e % 2
                if c == 0:
                    pe.wait_ge(wsplit, 4 * (2 * k + e) + 2)
                for f in range(FC):
                    if not (isinstance(k, int) and 4 * k + i == 0):
                        pe.wait_ge(gelu_done, 16 * k + 4 * (i - 1) + f + 1)
                    products(Hb[f], [[Ws[:, r, s, f * P:(f + 1) * P] for r in range(2)]],
                             [[xn2T[:, r, c * CH:(c + 1) * CH] for r in range(2)]]).then_inc(w1_done, 1)

            def down(k, i, fs=range(FC)):
                e, c = place(k, i)
                s = e % 2
                if c == 0:
                    pe.wait_ge(wsplit, 4 * (2 * k + e) + 4)
                pe.wait_ge(y_done, 4 * k + i + 1)
                for f in fs:
                    pe.wait_ge(h_lo, 16 * k + 4 * i + f + 1)
                    for n, (x_, y_) in enumerate(SPLIT):
                        last = pe.matmul(Yb[i % 2], Ws[:, x_, s, FF + f * P:FF + (f + 1) * P], Hs[:, y_, (i % 2) * FC + f, :],
                                         start=f == 0 and n == 0, stop=f == FC - 1 and n == len(SPLIT) - 1)
                if fs[-1] == FC - 1:
                    last.then_inc(w2_done, 1)

            pe.wait_ge(xn2T_lo, 1)
            outputs(1)
            gates_transposed(0)
            up(0, 0)
            up(0, 1)
            input_transposed(1, Rb)
            down(0, 0)
            pe.wait_ge(cwT_ok, 1)
            logits(1)
            up(0, 2)
            down(0, 1)
            down(0, 2)
            gates_transposed(1)
            up(0, 3)
            up(1, 0)
            down(0, 3)
            with pe.Fori(1, E // 2 - 1) as k:
                for i in range(4):
                    up(k, i + 1)
                    down(k, i)
            def sums_transposed(c, bank):
                pe.wait_ge(y_done, 2 * E + 2 - (CHUNKS - 1 - c))
                for t in range(CT):
                    last = pe.transpose(bank[:, t * P:(t + 1) * P], acc[:, (c * CT + t) * P:(c * CT + t + 1) * P], ident[:, :])
                last.then_inc(accT_mm, 1)

            for i in range(3):
                up(E // 2 - 1, i + 1)
                down(E // 2 - 1, i)
            down(E // 2 - 1, 3, range(FC - 1))
            sums_transposed(0, Ob)
            down(E // 2 - 1, 3, range(FC - 1, FC))
            sums_transposed(1, Rb)

        @block.vector
        def _(dve):
            links = [0]

            def link(ins):
                links[0] += 1
                ins.then_inc(dve_link, 1)
                dve.wait_ge(dve_link, links[0])

            dve.sem_inc(o_lo, 1)
            dve.sem_inc(y_done, 2)

            def lo_part(dst, full, hi):
                return dve.tensor_tensor(dst, full, hi.bitcast(F32), ALU.subtract)

            def statistics(src, ts, eps):
                for t in ts:
                    last = dve.bn_stats(st[:, t, :], src[:, t - ts[0], :])
                link(last)
                for t in ts:
                    last = dve.bn_aggr(mv[:, t, :], st[:, t, :])
                link(last)
                dve.tensor_scalar(ve[:, ts[0]:ts[-1] + 1], mv[:, ts[0]:ts[-1] + 1, 1], eps, None, ALU.add).then_inc(var_ok, 1)

            def normalize(dst, src, ts, n):
                dve.wait_ge(rstd_ok, n)
                for t in ts:
                    last = dve.tensor_scalar(dst[:, t - ts[0], :], src[:, t - ts[0], :], mv[:, t, 0:1], rstd[:, t:t + 1],
                                             ALU.subtract, ALU.mult)
                return last

            def normalized(ts, n):
                dve.wait_ge(rstd_ok, n)
                for t in ts:
                    dve.tensor_scalar(xn[:, t, :], x_sb[:, t, :], mv[:, t, 0:1], rstd[:, t:t + 1],
                                      ALU.subtract, ALU.mult).then_inc(xn_ok, 1)

            def xnT_part(i):
                (g0, g1), bank = XPARTS[i]
                cols = slice(g0 * N, g1 * N)
                dve.wait_ge(xnT_hi, i + 1)
                lo_part(xnT[:, 1, cols], bank, xnT[:, 0, cols]).then_inc(xnT_lo, 1)

            def wq_part(h):
                dve.wait_ge(wq_hi, h + 1)
                lo_part(wq_s[:, 1, PART[h]], wq_raw[:, PART[h]], wq_s[:, 0, PART[h]]).then_inc(wq_lo, 1)

            def wk_part(h):
                dve.wait_ge(wk_hi, h + 1)
                lo_part(wk_s[:, 1, :, PART[h]], wk_raw[:, :, PART[h]], wk_s[:, 0, :, PART[h]]).then_inc(wk_lo, 1)

            def null_key():
                dve.wait_ge(nk_prod, 1)
                link(dve.tensor_reduce(NKf[:], y_att[:, :, :].rearrange("p t n -> p (t n)").rearrange("p (h d) -> p h d", d=DH),
                                       AX.X, ALU.add))
                link(dve.tensor_copy(NK_s[:, 0, :], NKf[:]))
                lo_part(NK_s[:, 1, :], NKf[:], NK_s[:, 0, :]).then_inc(nk_lo, 1)

            def null_keys(ts):
                dve.wait_ge(ns_mm, ts[-1] // QT + 1)
                dve.tensor_scalar(nsn[:, ts[0]:ts[-1] + 1, :].rearrange("p t h -> p (t h)"),
                                  Rb[:, ts[0] * HEADS:(ts[-1] + 1) * HEADS], -SCALE, None, ALU.mult).then_inc(ns_ok, 1)

            dve.wait_ge(ld_x0, 16)
            statistics(x_sb[:, 0:QT, :], list(range(QT)), EPS_PRE)
            wq_part(0)
            normalized(range(QT), 1)
            for k in range(CK):
                dve.wait_ge(ctx0_hi, k + 1)
                lo_part(ctxT[:, 1, k, 0:M], ctx_raw[k][:, 0:M], ctxT[:, 0, k, 0:M]).then_inc(ctx0_lo, 1)
            xnT_part(0)
            wk_part(0)
            wq_part(1)

            def qk_part(b, c, bank):
                dve.wait_ge(qk_hi, UNITS * b + c + 1)
                lo_part(QK[:, 1, c, :], bank, QK[:, 0, c, :]).then_inc(qk_lo, 1)

            def null_scores(src, b, p):
                return src[:, bass.ds(QT * b, QT), 2 * p:2 * p + 2].rearrange("p t h -> p h t")

            def by_head(small, p):
                return small[:, p % 4, :].rearrange("p (h t) -> p h t", h=2)

            def maxima(new, old):
                if new:
                    b, p = new
                    dve.wait_ge(s_done, UNITS * b + p + 1)
                    dve.tensor_reduce(mx[:, p % 4, :], S[:, p % 2, :, :].rearrange("p h (t m) -> p (h t) m", m=M), AX.X, ALU.max,
                                      negate=True).then_inc(mx_ok, 1)
                if old:
                    c, r = old
                    dve.wait_ge(exp_done, UNITS * c + r + 1)
                    dve.tensor_tensor(den[:, r % 4, :], sm[:, r % 4, :], en[:, r % 4, :], ALU.add).then_inc(den_ok, 1)
                if new:
                    dve.wait_ge(mx_ok, UNITS * b + p + 1)
                    dve.scalar_tensor_tensor(by_head(nm, p), by_head(mx, p), SCALE, null_scores(nsn, b, p),
                                             ALU.mult, ALU.min).then_inc(nm_ok, 1)
                if old:
                    dve.wait_ge(den_ok, UNITS * c + r + 1)
                    dve.reciprocal(rden[:, r % 4, :], den[:, r % 4, :]).then_inc(rden_ok, 1)
                if new:
                    dve.wait_ge(nm_ok, UNITS * b + p + 1)
                    dve.tensor_tensor(by_head(t4, p), by_head(nm, p), null_scores(nsn, b, p), ALU.subtract).then_inc(t4_ok, 1)
                if old:
                    dve.wait_ge(rden_ok, UNITS * c + r + 1)
                    dve.tensor_tensor(null_scores(pn, c, r), by_head(en, r), by_head(rden, r), ALU.mult).then_inc(pn_ok, 1)

            def probabilities(b, p):
                dve.wait_ge(t_done, UNITS * b + p + 1)
                dve.tensor_copy(PT[:, p % 2, 0, :], Tb[:, 0, :]).then_inc(pt_sb, 1)

            def o_part(b, p):
                dve.wait_ge(o_hi, UNITS * b + p + 1)
                lo_part(O[:, 1, p, :], Ob[:, 0:N], O[:, 0, p, :]).then_inc(o_lo, 1)

            qk_part(0, 0, lead_banks[0])
            null_key()
            wk_part(1)
            dve.wait_ge(const_ok, 4)
            for h in range(2):
                rows = slice(h * DH, (h + 1) * DH)
                flat = NVB[rows, :, :].rearrange("p c h -> p (c h)")
                dve.tensor_copy(flat[:, h:(PAIRS - 1) * (HEADS + 2) + h + 1:HEADS + 2],
                                nv_col[rows, 0:1].to_broadcast([DH, PAIRS])).then_inc(nvb_ok, 1)

            null_keys(range(QT))
            qk_part(0, 1, lead_banks[1])
            maxima((0, 0), None)
            dve.wait_ge(ld_x, 16)
            statistics(x_sb[:, QT:TILES, :], list(range(QT, TILES)), EPS_PRE)
            qk_part(0, 2, lead_banks[2])
            qk_part(0, 3, lead_banks[3])
            normalized(range(QT, TILES), 2)
            maxima((0, 1), (0, 0))
            qk_part(0, 4, lead_banks[4])
            qk_part(0, 5, lead_banks[5])
            dve.wait_ge(nw_mm, 1)
            dve.tensor_copy(NW[:, :], Rb[0:HEADS, 0:DIM]).then_inc(nw_sb, 1)
            qk_part(0, 6, lead_banks[6])
            xnT_part(1)
            qk_part(0, 7, lead_banks[7])
            xnT_part(2)
            maxima((0, 2), (0, 1))
            probabilities(0, 0)
            maxima((0, 3), (0, 2))
            probabilities(0, 1)
            null_keys(range(QT, TILES))
            def scaled_norm(dst, src, ts, w):
                for n, t in enumerate(ts):
                    last = dve.scalar_tensor_tensor(dst[:, n, :], src[:, n, :], mv[:, t, 0:1], w, ALU.subtract, ALU.mult)
                link(last)

            def residual(dst, plus, ts, n):
                dve.wait_ge(rstd_ok, n)
                for i, t in enumerate(ts):
                    last = dve.scalar_tensor_tensor(dst[:, i, :], dst[:, i, :], rstd[:, t:t + 1], plus[:, i, :],
                                                    ALU.mult, ALU.add)
                return last

            link(dve.tensor_copy(rw_s[:, 0, :], rw_f))
            lo_part(rw_s[:, 1, :], rw_f, rw_s[:, 0, :]).then_inc(rw_lo, 1)

            def null_transposed(c, bank):
                dve.wait_ge(pnT_mm, c + 1)
                dve.tensor_copy(pnT[:, :], bank[0:HEADS, :]).then_inc(pnT_sb, 1)

            def output_statistics(c):
                dve.wait_ge(y_mm, c + 1)
                statistics(Rb[:, :].rearrange("p (t n) -> p t n", t=CT), list(range(c * CT, (c + 1) * CT)), EPS_ATT)

            def attended(c):
                t, ts = slice(c * CT, (c + 1) * CT), list(range(c * CT, (c + 1) * CT))
                scaled_norm(x1[:, t, :], Rb[:, :].rearrange("p (t n) -> p t n", t=CT), ts, l1w)
                dve.wait_ge(xb_ok, 1)
                residual(x1[:, t, :], x_sb[:, t, :], ts, NORMS + 1 + 2 * c).then_inc(x1_ok, 1)

            def input_statistics(c):
                dve.wait_ge(x1_ok, c + 1)
                statistics(x1[:, c * CT:(c + 1) * CT, :], list(range(c * CT, (c + 1) * CT)), EPS_PRE)

            def experts_input(c):
                t, ts = slice(c * CT, (c + 1) * CT), list(range(c * CT, (c + 1) * CT))
                normalize(xn2[:, t, :], x1[:, t, :], ts, NORMS + 2 + 2 * c).then_inc(xn2_ok, 1)

            def input_transposed(c, bank):
                tok = slice(c * CH, (c + 1) * CH)
                dve.wait_ge(acc_ok, c + 1)
                lo_part(xn2T[:, 1, tok], bank[:, :], xn2T[:, 0, tok]).then_inc(xn2T_lo, 1)

            def largest(c):
                dve.wait_ge(lg_mm, c + 1)
                dve.tensor_tensor(lg[:], Ob[:, 0:CT * E].rearrange("p (t e) -> p t e", t=CT),
                                  rb_b[:, None, :].to_broadcast([P, CT, E]), ALU.add).then_inc(lg_ok, 1)
                dve.wait_ge(lg_ok, c + 1)
                for i in range(CT):
                    last = dve.max(top[:, i, :], lg[:, i, :])
                link(last)
                dve.tensor_tensor(gd[:], top[:, :, 1], top[:, :, 0], ALU.subtract).then_inc(gap_ok, 1)
                for i in range(CT):
                    last = dve.max_index(topi[:, i, :], top[:, i, :], lg[:, i, :])
                link(last)
                link(dve.tensor_copy(topf[:], topi[:]))

            def gates(c):
                dve.wait_ge(ge_ok, c + 1)
                link(dve.tensor_scalar(g1[:], ge[:], 1.0, None, ALU.add))
                link(dve.reciprocal(gw0[:], g1[:]))
                link(dve.tensor_tensor(gw1[:], ge[:], gw0[:], ALU.mult))
                for i in range(CT):
                    dve.tensor_scalar(ca[:, i, :], iota8[:], topf[:, i, 0:1], gw0[:, i:i + 1], ALU.is_equal, ALU.mult)
                    last = dve.tensor_scalar(cb[:, i, :], iota8[:], topf[:, i, 1:2], gw1[:, i:i + 1], ALU.is_equal, ALU.mult)
                link(last)
                dve.tensor_tensor(cw[:], ca[:], cb[:], ALU.add).then_inc(cw_ok, 1)

            def gates_transposed(c):
                dve.wait_ge(cwT_mm, c + 1)
                if c:
                    dve.wait_ge(cw_st, 16 * c)
                dve.tensor_copy(cwT[:, :], Ob[0:E, :]).then_inc(cwT_ok, 1)

            def body(b, last):
                def unit(p):
                    return (b, p) if p < UNITS else None if last else (b + 1, p - UNITS)

                for p in range(1, UNITS):
                    o_part(b, p - 1)
                    maxima(unit(p + 3), unit(p + 2))
                    with_values = p in (1, 2) or p in (5, 6) and not last
                    copies = unit(p + 1) and not (last and p + 1 >= BOTH)
                    if with_values and copies:
                        probabilities(*unit(p + 1))
                    if not last:
                        qk_part(b + 1, p - 1, Rb[:, :])
                    if not with_values and copies:
                        probabilities(*unit(p + 1))
                    if last:
                        if p == 1:
                            null_transposed(0, Rb)
                        elif p == 3:
                            output_statistics(0)
                        elif p == 4:
                            attended(0)
                        elif p == 5:
                            input_statistics(0)
                        elif p == 6:
                            experts_input(0)
                        elif p == 7:
                            input_transposed(0, Rb)
                o_part(b, UNITS - 1)
                if not last:
                    maxima((b + 1, 3), (b + 1, 2))
                    probabilities(b + 1, 1)
                    qk_part(b + 1, UNITS - 1, Rb[:, :])

            with dve.Fori(0, B - 1) as b:
                body(b, False)
            body(B - 1, True)

            def hidden(k, i, fs=range(FC)):
                for f in fs:
                    slot = (i % 2) * FC + f
                    if f < FC - 1:
                        dve.wait_ge(h_hi, 12 * k + 3 * i + f + 1)
                    else:
                        dve.wait_ge(gelu_done, 16 * k + 4 * i + FC)
                        dve.tensor_copy(Hs[:, 0, slot, :], Hf[:, f, :]).then_inc(h_hi3, 1)
                        dve.wait_ge(h_hi3, 4 * k + i + 1)
                    lo_part(Hs[:, 1, slot, :], Hf[:, f, :], Hs[:, 0, slot, :]).then_inc(h_lo, 1)

            def gather(k, i):
                e, c = place(k, i)
                dve.wait_ge(cwB_ok[i % 2], 32 * k + 16 * (i // 2 + 1))
                dve.wait_ge(w2_done, 4 * k + i + 2)
                dve.wait_ge(y_done, 4 * k + i + 2)
                dve.scalar_tensor_tensor(tmp[:], Yb[i % 2], b2_sb[:, bass.ds(2 * k + e, 1)], cwB[:, i % 2, :],
                                         ALU.add, ALU.mult).then_inc(y_part, 1)
                if isinstance(k, int) and k == 0:
                    dve.wait_ge(acc_ok, c + 1)
                dve.wait_ge(y_part, 4 * k + i + 1)
                part = acc[:, c * CH:(c + 1) * CH]
                dve.tensor_tensor(part, part, tmp[:], ALU.add).then_inc(y_done, 1)

            null_transposed(1, S[:, 0, 0, :])
            largest(0)
            gates(0)
            output_statistics(1)
            gates_transposed(0)
            attended(1)
            input_statistics(1)
            hidden(0, 0, (0, 1))
            experts_input(1)
            hidden(0, 0, (2, 3))
            input_transposed(1, Rb)
            hidden(0, 1)
            gather(0, 0)
            largest(1)
            hidden(0, 2)
            gates(1)
            gather(0, 1)
            gates_transposed(1)
            hidden(0, 3)
            hidden(1, 0, (0, 1))
            gather(0, 2)
            hidden(1, 0, (2, 3))
            gather(0, 3)
            with dve.Fori(1, E // 2 - 1) as k:
                for i in range(4):
                    hidden(k, i + 1)
                    gather(k, i)
            for i in range(3):
                hidden(E // 2 - 1, i + 1)
                gather(E // 2 - 1, i)

            def sums(c):
                return (Ob, Rb)[c][:, :].rearrange("p (t n) -> p t n", t=CT)

            def sum_statistics(c):
                dve.wait_ge(accT_mm, c + 1)
                statistics(sums(c), list(range(c * CT, (c + 1) * CT)), EPS_MOE)

            def result(c):
                t, ts = slice(c * CT, (c + 1) * CT), list(range(c * CT, (c + 1) * CT))
                scaled_norm(y_att[:, t, :], sums(c), ts, l2w)
                dve.wait_ge(xb_ok, 2)
                residual(y_att[:, t, :], x_sb[:, t, :], ts, NORMS + 1 + 2 * CHUNKS + c).then_inc(res_ok, 1)

            sum_statistics(0)
            gather(E // 2 - 1, 3)
            result(0)
            sum_statistics(1)
            result(1)


def kernel(**inputs):
    import numpy as np
    import concourse.bacc as bacc
    from concourse.bass_utils import run_bass_kernel_spmd

    a = {k: np.asarray(v) for k, v in inputs.items()}
    wkv = a["L0_xattn_Wkv"]

    def tiles(w):
        return w.reshape(-1, P, w.shape[1]).transpose(1, 0, 2)

    w1, w2 = a["L0_ffn_w1"], a["L0_ffn_w2"]
    laid = {
        "x": a["x"].reshape(TILES, P, DIM).transpose(1, 0, 2),
        "ctx_t": tiles(a["ctx_2048"].reshape(B * M, CTX).T),
        "wq": a["L0_xattn_Wq"],
        "wk": tiles(wkv[:, :INNER]),
        "wv": tiles(wkv[:, INNER:]),
        "wout": tiles(a["L0_xattn_Wout"]),
        "rows": np.concatenate([a["L0_xattn_ln_scale"], a["L0_xattn_ln_bias"], a["L0_ffn_ln_w"], a["L0_ffn_ln_b"],
                                a["L0_ffn_router_b"], a["L0_xattn_null_kv"][0]])[None],
        "columns": np.concatenate([a["L0_ffn_b1"].reshape(E * FC, P).T, a["L0_ffn_b2"].T, a["L0_ffn_router_w"].T,
                                   np.concatenate([a["L0_xattn_null_kv"][1]] * 2)[:, None]], axis=1),
        "w1_t": w1.transpose(0, 2, 1),
        "w2_t": w2.reshape(E, DIM, FC, P).transpose(0, 3, 2, 1).reshape(E, P, FF),
    }
    laid = {k: np.ascontiguousarray(v) for k, v in laid.items()}
    nc = bacc.Bacc("TRN2", target_bir_lowering=False, num_devices=1)
    args = {k: nc.dram_tensor(f"in_{k}", v.shape, mybir.dt.from_np(v.dtype), kind="ExternalInput").ap() for k, v in laid.items()}
    out = nc.dram_tensor("out_0", (P, TILES, DIM), F32, kind="ExternalOutput").ap()
    build(nc, *args.values(), out)
    r = run_bass_kernel_spmd(nc, [{f"in_{k}": v for k, v in laid.items()}], core_ids=[0])
    got = r.results[0]["out_0"]
    return got.transpose(1, 0, 2).reshape(B, N, DIM)
```

```python
import math
from contextlib import ExitStack

import concourse.bass as bass
from concourse import mybir

F32 = mybir.dt.float32
F32R = mybir.dt.float32r
U32 = mybir.dt.uint32
ALU = mybir.AluOpType
ACT = mybir.ActivationFunctionType
AX = mybir.AxisListType

P = 128
B, N, DIM = 4, 256, 128
M, CTX = 256, 256
HEADS, DH = 16, 64
INNER = HEADS * DH
PAIRS = HEADS // 2
UNITS = PAIRS
QT = N // P
KT = M // P
CK = CTX // P
TOK = B * N
TILES = TOK // P
E, FF = 8, 512
FC = FF // P
CH = 512
CHUNKS = TOK // CH
CT = CH // P
VP = 4
SCALE = DH ** -0.5
NORMS = 2
EPS_PRE, EPS_ATT, EPS_MOE = 1e-5, 1e-6, 1e-12
ROWS = 4 * DIM + E + DH
COLS = E * FC + 2 * E + 1
PART = (slice(0, 2 * P), slice(2 * P, INNER))
BOTH = (4, 5, 6, 7)
SPLIT = ((0, 0), (0, 1), (1, 0))


def build(nc, x, ctx_t, wq, wk, wv, wout, rows, columns, w1_t, w2_t, out):
    stack = ExitStack()
    with stack:
        def sb(name, shape, dt=F32):
            return stack.enter_context(nc.sbuf_tensor(name, shape, dt))

        def sem(name):
            return stack.enter_context(nc.semaphore(name))

        x_sb = sb("x_sb", [P, TILES, DIM])
        xn = sb("xn", [P, TILES, DIM])
        x1 = xn
        xnT = sb("xnT", [P, 2, TOK], F32R)
        wq_s = sb("wq_s", [P, 2, INNER], F32R)
        wk_s = sb("wk_s", [P, 2, CK, INNER], F32R)
        wv_s = sb("wv_s", [P, 2, CK, INNER], F32R)
        wout_s = sb("wout_s", [P, 2, PAIRS, DIM], F32R)
        ctxT = sb("ctxT", [P, 2, CK, TOK], F32R)
        ctxV = sb("ctxV", [P, 2, CK, M], F32R)
        QK = sb("QK", [P, 2, UNITS, N + M], F32R)
        Hs = QK
        V = sb("V", [P, KT, INNER])
        Hf = V[:, :, :].rearrange("p k (f n) -> p (k f) n", n=CH)
        wq_raw = V[:, 0, :]
        Pr = sb("Pr", [P, 2, 2, QT, M])
        cwB = Pr[:, 0, :, :, :].rearrange("p h t m -> p (h t m)").rearrange("p (s n) -> p s n", s=2)
        PT = sb("PT", [P, 2, 2, KT * N])
        wk_raw = PT[:, :, :, :].rearrange("p a h n -> p (a h n)").rearrange("p (k n) -> p k n", k=CK)
        O = sb("O", [P, 2, UNITS, N], F32R)
        y_att = sb("y_att", [P, TILES, DIM])
        yT = sb("yT", [P, TOK])
        xn2 = sb("xn2", [P, TILES, DIM])
        ctx_raw = [yT[:, :], xn2[:, :, :].rearrange("p t n -> p (t n)")]
        xn2T = sb("xn2T", [P, 2, TOK], F32R)
        Wraw = sb("Wraw", [P, 2, 2, FF])
        wv_raw = Wraw[:, :, :, :].rearrange("p s w n -> p (s w n)").rearrange("p (k n) -> p k n", k=CK)
        Ws = wk_s
        acc = sb("acc", [P, TOK])
        wout_raw = acc[:, :].rearrange("p (c n) -> p c n", c=PAIRS)
        tmp = sb("tmp", [P, CH])
        ident = sb("ident", [P, P])
        rows_b = sb("rows_b", [P, ROWS])
        l1w, l1b, l2w, l2b = (rows_b[:, i * DIM:(i + 1) * DIM] for i in range(4))
        rb_b, nk_b = rows_b[:, 4 * DIM:4 * DIM + E], rows_b[:, 4 * DIM + E:ROWS]
        cols_sb = sb("cols_sb", [P, COLS])
        b1_sb, b2_sb, rw_f, nv_col = (cols_sb[:, a:b] for a, b in ((0, E * FC), (E * FC, E * FC + E),
                                                                   (E * FC + E, E * FC + 2 * E), (COLS - 1, COLS)))
        NVB = sb("NVB", [P, PAIRS, HEADS])
        NKf = sb("NKf", [P, HEADS])
        NK_s = sb("NK_s", [P, 2, HEADS], F32R)
        NW = sb("NW", [HEADS, DIM])
        nsn = sb("nsn", [P, TILES, HEADS])
        pn = sb("pn", [P, TILES, HEADS])
        pnT = sb("pnT", [HEADS, CH])
        mx = sb("mx", [P, 4, 4])
        nm = sb("nm", [P, 4, 4])
        t4 = sb("t4", [P, 4, 4])
        en = sb("en", [P, 4, 4])
        sm = sb("sm", [P, 4, 4])
        den = sb("den", [P, 4, 4])
        rden = sb("rden", [P, 4, 4])
        st = sb("st", [P, TILES, 6])
        mv = sb("mv", [P, TILES, 2])
        ve = sb("ve", [P, TILES])
        rstd = sb("rstd", [P, TILES])
        mhalf = sb("mhalf", [P, TILES])
        spare = sb("spare", [P, 1])
        euler = sb("euler", [P, CT])
        iota8 = sb("iota8", [P, E])
        rw_s = sb("rw_s", [P, 2, E], F32R)
        lg = sb("lg", [P, CT, E])
        top = sb("top", [P, CT, E])
        topi = sb("topi", [P, CT, E], U32)
        topf = sb("topf", [P, CT, E])
        gd = sb("gd", [P, CT])
        ge = sb("ge", [P, CT])
        g1 = sb("g1", [P, CT])
        gw0 = sb("gw0", [P, CT])
        gw1 = sb("gw1", [P, CT])
        ca = sb("ca", [P, CT, E])
        cb = sb("cb", [P, CT, E])
        cw = sb("cw", [P, CT, E])
        cwT = sb("cwT", [E, CH])
        cw_dram = nc.dram_tensor("cw_scratch", (E, TOK), F32, kind="Internal").ap()

        S = stack.enter_context(nc.psum_tensor("S", [P, 2, 2, QT * M], F32))
        Tb = stack.enter_context(nc.psum_tensor("Tb", [P, 2, KT * N], F32))
        Ob = stack.enter_context(nc.psum_tensor("Ob", [P, 512], F32))
        Rb = stack.enter_context(nc.psum_tensor("Rb", [P, 512], F32))
        lead_banks = [(Tb[:, 0, :], Tb[:, 1, :], Ob[:, :])[c % 3] for c in range(UNITS)]
        XPARTS = [((0, 1), S[:, 1, 1, 0:N]), ((1, 3), Rb[:, :]), ((3, 4), Ob[:, 0:N])]
        Hb = [S[:, 0, 0, :], S[:, 0, 1, :], S[:, 1, 0, :], S[:, 1, 1, :]]
        Yb = [Tb[:, 0, :], Tb[:, 1, :]]
        GROUPS = [range(0, CT), range(CT, CT + QT), range(CT + QT, TILES)]
        ENDS = [(range(0, CT), Ob), (range(CT, CT + 2), Rb), (range(CT + 2, TILES), S[:, 0, 0, :])]

        ld_x0, ld_x, ld_ctx0, ld_ctx1, ld_wout, ld_small = (
            sem(n) for n in ("ld_x0", "ld_x", "ld_ctx0", "ld_ctx1", "ld_wout", "ld_small"))
        ld_wq, ld_wk, ld_wv = ([sem(f"ld_{n}{h}") for h in range(2)] for n in ("wq", "wk", "wv"))
        ident_ok, const_ok = sem("ident_ok"), sem("const_ok")
        var_ok, rstd_ok, xn_ok = sem("var_ok"), sem("rstd_ok"), sem("xn_ok")
        xnT_mm, xnT_hi, xnT_lo = sem("xnT_mm"), sem("xnT_hi"), sem("xnT_lo")
        wq_hi, wq_lo, wk_hi, wk_lo, wv_hi, wv_lo = (sem(n) for n in ("wq_hi", "wq_lo", "wk_hi", "wk_lo", "wv_hi", "wv_lo"))
        ctx0_hi, ctx0_lo, ctx1_hi, ctx1_lo, wout_hi, wout_lo, ctxV_ok = (
            sem(n) for n in ("ctx0_hi", "ctx0_lo", "ctx1_hi", "ctx1_lo", "wout_hi", "wout_lo", "ctxV_ok"))
        nk_prod, nk_lo, ns_mm, ns_ok = (sem(n) for n in ("nk_prod", "nk_lo", "ns_mm", "ns_ok"))
        qk_mm, qk_hi, qk_lo = sem("qk_mm"), sem("qk_hi"), sem("qk_lo")
        v_mm, v_sb = sem("v_mm"), sem("v_sb")
        s_done, mx_ok, nm_ok, t4_ok, exp_done = (sem(n) for n in ("s_done", "mx_ok", "nm_ok", "t4_ok", "exp_done"))
        den_ok, rden_ok, pn_ok, scaled = (sem(n) for n in ("den_ok", "rden_ok", "pn_ok", "scaled"))
        t_done, pt_sb, pt_sb2, pv_done, o_hi, o_lo = (sem(n) for n in ("t_done", "pt_sb", "pt_sb2", "pv_done", "o_hi", "o_lo"))
        out_mm, y_sb = sem("out_mm"), sem("y_sb")
        nvb_ok, nw_mm, nw_sb, pnT_mm, pnT_sb, x1_ok, xn2_ok, xn2T_mm, xn2T_hi, xn2T_lo, y_mm = (
            sem(n) for n in ("nvb_ok", "nw_mm", "nw_sb", "pnT_mm", "pnT_sb", "x1_ok", "xn2_ok", "xn2T_mm", "xn2T_hi", "xn2T_lo", "y_mm"))
        rw_lo, lg_mm, lg_ok, gap_ok, ge_ok, cw_ok, cwT_mm, cwT_ok, accT_mm, res_ok, dve_link, h_hi3 = (
            sem(n) for n in ("rw_lo", "lg_mm", "lg_ok", "gap_ok", "ge_ok", "cw_ok", "cwT_mm", "cwT_ok", "accT_mm", "res_ok", "dve_link", "h_hi3"))
        acc_ok, xb_ok = sem("acc_ok"), sem("xb_ok")
        cw_st, cwB_ok = sem("cw_st"), [sem("cwB_ok0"), sem("cwB_ok1")]
        wraw_ok, wsplit = [sem("wraw_ok0"), sem("wraw_ok1")], sem("wsplit")
        w1_done, gelu_done, h_hi, h_lo, w2_done, y_part, y_done = (
            sem(n) for n in ("w1_done", "gelu_done", "h_hi", "h_lo", "w2_done", "y_part", "y_done"))
        store = sem("store")
        pool_past, act_past = sem("pool_past"), sem("act_past")

        def peeled(k):
            return isinstance(k, int)

        def first_pair(k):
            return peeled(k) and k == 0

        def place(k, i):
            return (i % 2, i // 2) if first_pair(k) else (i // CHUNKS, i % CHUNKS)

        block = stack.enter_context(nc.Block())

        @block.sync
        def _(sp):
            sp.dma_start(x_sb[:, 0:QT, :], x[:, 0:QT, :]).then_inc(ld_x0, 16)
            half = [slice(h * INNER // 2, (h + 1) * INNER // 2) for h in range(2)]
            sp.dma_start(wq_raw[:, PART[0]], wq[:, PART[0]]).then_inc(ld_wq[0], 16)
            for k in range(CK):
                sp.dma_start(ctx_raw[k][:, 0:M], ctx_t[:, k, 0:M]).then_inc(ld_ctx0, 16)
            sp.dma_start(wk_raw[:, :, PART[0]], wk[:, :, PART[0]]).then_inc(ld_wk[0], 16)
            sp.dma_start(wq_raw[:, PART[1]], wq[:, PART[1]]).then_inc(ld_wq[1], 16)
            sp.dma_start(wk_raw[:, :, PART[1]], wk[:, :, PART[1]]).then_inc(ld_wk[1], 16)
            sp.dma_start(x_sb[:, QT:TILES, :], x[:, QT:TILES, :]).then_inc(ld_x, 16)
            sp.dma_start(wv_raw[:, :, half[0]], wv[:, :, half[0]]).then_inc(ld_wv[0], 16)
            for k in range(CK):
                sp.dma_start(ctx_raw[k][:, M:TOK], ctx_t[:, k, M:TOK]).then_inc(ld_ctx1, 16)
            sp.dma_start(wv_raw[:, :, half[1]], wv[:, :, half[1]]).then_inc(ld_wv[1], 16)
            sp.dma_start(wout_raw, wout).then_inc(ld_wout, 16)

            def load_expert(e, s):
                sp.dma_start(Wraw[:, s, 0, :], w1_t[bass.ds(e, 1), :, :].rearrange("e p n -> p (e n)")).then_inc(wraw_ok[s], 16)
                sp.dma_start(Wraw[:, s, 1, :], w2_t[bass.ds(e, 1), :, :].rearrange("e p n -> p (e n)")).then_inc(wraw_ok[s], 16)

            def gate(e, c, s):
                sp.dma_start(cwB[:, s, :], cw_dram[bass.ds(e, 1), c * CH:(c + 1) * CH].to_broadcast([P, CH])).then_inc(cwB_ok[s], 16)

            sp.wait_ge(wv_hi, 2)
            sp.wait_ge(wv_lo, 2)
            load_expert(0, 0)
            load_expert(1, 1)
            def store_gates(c):
                sp.wait_ge(cwT_ok, c + 1)
                sp.dma_start(cw_dram[:, c * CH:(c + 1) * CH], cwT[:, :]).then_inc(cw_st, 16)
                sp.wait_ge(cw_st, 16 * (c + 1))

            def gates(k, i):
                e, c = place(k, i)
                if not (first_pair(k) and i < 2):
                    sp.wait_ge(y_done, 4 * k + i + 1)
                gate(2 * k + e, c, i % 2)

            for e in range(2, 4):
                sp.wait_ge(wsplit, 4 * (e - 1))
                load_expert(e, e % 2)
            store_gates(0)
            gates(0, 0)
            gates(0, 1)
            store_gates(1)
            gates(0, 2)
            gates(0, 3)
            with sp.Fori(1, E // 2 - 1) as k:
                for s in range(2):
                    sp.wait_ge(wsplit, 4 * (2 * k + s + 1))
                    load_expert(2 * k + s + 2, s)
                    gates(k, 2 * s)
                    gates(k, 2 * s + 1)
            for i in range(4):
                gates(E // 2 - 1, i)
            for n, (ts, _) in enumerate(ENDS):
                sp.wait_ge(res_ok, n + 1)
                sp.dma_start(out[:, ts[0]:ts[-1] + 1, :], y_att[:, ts[0]:ts[-1] + 1, :]).then_inc(store, 16)
            sp.wait_ge(store, 16 * len(ENDS))

        @block.gpsimd
        def _(pool):
            pool.memset(ident[:], 0.0).then_inc(ident_ok, 1)
            pool.wait_ge(ident_ok, 1)
            pool.affine_select(out=ident[:], in_=ident[:], compare_op=ALU.not_equal, fill=1.0, base=0,
                               pattern=[[-1, P]], channel_multiplier=1).then_inc(ident_ok, 1)
            pool.memset(mhalf[:], -0.5).then_inc(const_ok, 1)
            pool.memset(euler[:], math.e).then_inc(const_ok, 1)
            pool.iota(iota8[:], pattern=[[1, E]], base=0, channel_multiplier=0,
                      allow_small_or_imprecise_dtypes=True).then_inc(const_ok, 1)
            pool.memset(NVB[:], 0.0).then_inc(const_ok, 1)
            pool.wait_ge(const_ok, 1)
            pool.wait_ge(var_ok, 1)
            pool.tensor_tensor(rstd[:, 0:QT], ve[:, 0:QT], mhalf[:, 0:QT], ALU.pow).then_inc(rstd_ok, 1)
            for h in range(2):
                pool.wait_ge(ld_wq[h], 16)
            pool.wait_ge(ld_small, 32)
            pool.tensor_tensor(y_att[:, :, :].rearrange("p t n -> p (t n)").rearrange("p (h d) -> p h d", d=DH),
                               wq_raw.rearrange("p (h d) -> p h d", d=DH),
                               nk_b[:, None, :].to_broadcast([P, HEADS, DH]), ALU.mult).then_inc(nk_prod, 1)
            pool.wait_ge(ctx0_lo, CK)
            for r in range(2):
                pool.tensor_copy(ctxV[:, r, :, :], ctxT[:, r, :, 0:M]).then_inc(ctxV_ok, 1)

            def wv_part(h):
                cols = slice(h * INNER // 2, (h + 1) * INNER // 2)
                pool.wait_ge(wv_hi, h + 1)
                pool.tensor_tensor(wv_s[:, 1, :, cols], wv_raw[:, :, cols], wv_s[:, 0, :, cols].bitcast(F32),
                                   ALU.subtract).then_inc(wv_lo, 1)

            def scale(b, p):
                pool.wait_ge(rden_ok, UNITS * b + p + 1)
                pool.sem_inc(pool_past, 1)
                for h in range(2):
                    for q in range(QT):
                        last = pool.tensor_scalar(Pr[:, p % 2, h, q, :], Pr[:, p % 2, h, q, :],
                                                  rden[:, p % 4, h * QT + q:h * QT + q + 1], 1.0, ALU.mult, ALU.mult)
                last.then_inc(scaled, 1)

            def ctx_part(k):
                pool.wait_ge(ctx1_hi, k + 1)
                pool.tensor_tensor(ctxT[:, 1, k, M:TOK], ctx_raw[k][:, M:TOK], ctxT[:, 0, k, M:TOK].bitcast(F32),
                                   ALU.subtract).then_inc(ctx1_lo, 1)

            wv_part(0)
            ctx_part(0)
            pool.wait_ge(var_ok, 2)
            pool.tensor_tensor(rstd[:, QT:TILES], ve[:, QT:TILES], mhalf[:, QT:TILES], ALU.pow).then_inc(rstd_ok, 1)
            ctx_part(1)
            scale(0, 0)
            wv_part(1)
            scale(0, 1)
            scale(0, 2)
            pool.wait_ge(wout_hi, 1)
            pool.tensor_tensor(wout_s[:, 1, :, :], wout_raw, wout_s[:, 0, :, :].bitcast(F32), ALU.subtract).then_inc(wout_lo, 1)

            pool.tensor_tensor(x_sb[:], x_sb[:], l1b[:, None, :].to_broadcast([P, TILES, DIM]), ALU.add).then_inc(xb_ok, 1)

            def split(e, s, ws=(0, 1)):
                for w in ws:
                    hi, lo = (Ws[:, r, s, w * FF:(w + 1) * FF] for r in range(2))
                    pool.tensor_scalar(hi, Wraw[:, s, w, :], 1.0, 1.0, ALU.mult, ALU.mult).then_inc(wsplit, 1)
                    pool.wait_ge(wsplit, 4 * e + 2 * w + 1)
                    pool.tensor_tensor(lo, Wraw[:, s, w, :], hi.bitcast(F32), ALU.subtract).then_inc(wsplit, 1)

            def power(ts, count):
                t = slice(ts[0], ts[-1] + 1)
                pool.wait_ge(var_ok, count)
                pool.tensor_tensor(rstd[:, t], ve[:, t], mhalf[:, t], ALU.pow).then_inc(rstd_ok, 1)

            def tail_power(g, n):
                power(GROUPS[g], NORMS + 2 * g + n + 1)

            def gap(c):
                pool.wait_ge(gap_ok, c + 1)
                pool.tensor_tensor(ge[:], euler[:], gd[:], ALU.pow).then_inc(ge_ok, 1)

            def body(b, last):
                for p in range(1, UNITS):
                    if p + 2 < UNITS:
                        scale(b, p + 2)
                    elif not last:
                        scale(b + 1, p + 2 - UNITS)
                    if p in (2, 3) and not last:
                        if p == 2:
                            pool.wait_ge(v_mm, VP * (b + 1))
                            pool.sem_inc(pool_past, 1)
                        pool.tensor_copy(ctxV[:, p - 2, :, :],
                                         ctxT[:, p - 2, :, bass.ds((b + 1) * M, M)]).then_inc(ctxV_ok, 1)
                    if last and p in (3, 5):
                        tail_power(0, (p - 3) // 2)
                    if last and p in (1, 2, 6):
                        if p == 1:
                            pool.wait_ge(qk_mm, UNITS * B)
                        if p in (1, 6):
                            pool.wait_ge(wraw_ok[p // 6], 32)
                        split(p // 6, p // 6, {1: (0,), 2: (1,), 6: (0, 1)}[p])
                if not last:
                    scale(b + 1, 2)

            with pool.Fori(0, B - 1) as b:
                body(b, False)
            body(B - 1, True)

            tail_power(1, 0)
            tail_power(1, 1)
            gap(0)
            tail_power(2, 0)
            tail_power(2, 1)
            gap(1)
            for e in range(2, 4):
                pool.wait_ge(w2_done, e + 2)
                pool.wait_ge(wraw_ok[e % 2], 64)
                split(e, e % 2)
            pool.wait_ge(x1_ok, len(GROUPS))
            pool.wait_ge(xn2_ok, len(GROUPS))
            pool.tensor_tensor(x_sb[:], x1[:], l2b[:, None, :].to_broadcast([P, TILES, DIM]), ALU.add).then_inc(xb_ok, 1)
            with pool.Fori(2, E // 2) as k:
                for s in range(2):
                    pool.wait_ge(w2_done, 4 * k + 2 * s - 1)
                    pool.wait_ge(wraw_ok[s], 32 * (k + 1))
                    pool.sem_inc(pool_past, 1)
                    split(2 * k + s, s)
            for n, (ts, _) in enumerate(ENDS):
                power(ts, NORMS + 2 * len(GROUPS) + n + 1)

        @block.scalar
        def _(act):
            act.dma_start(rows_b[:], rows.to_broadcast([P, ROWS])).then_inc(ld_small, 16)
            act.dma_start(cols_sb[:], columns).then_inc(ld_small, 16)
            half = [slice(h * INNER // 2, (h + 1) * INNER // 2) for h in range(2)]

            def hi_part(dst, full, done):
                act.activation(dst, full, ACT.Copy).then_inc(done, 1)

            def ctx_part(loaded, cols, done):
                act.wait_ge(loaded, 16 * CK)
                for k in range(CK):
                    hi_part(ctxT[:, 0, k, cols], ctx_raw[k][:, cols], done)

            def wq_part(h):
                act.wait_ge(ld_wq[h], 16)
                hi_part(wq_s[:, 0, PART[h]], wq_raw[:, PART[h]], wq_hi)

            def wk_part(h):
                act.wait_ge(ld_wk[h], 16)
                hi_part(wk_s[:, 0, :, PART[h]], wk_raw[:, :, PART[h]], wk_hi)

            def wv_part(h):
                act.wait_ge(ld_wv[h], 16)
                hi_part(wv_s[:, 0, :, half[h]], wv_raw[:, :, half[h]], wv_hi)

            def xnT_part(i):
                (g0, g1), bank = XPARTS[i]
                act.wait_ge(xnT_mm, i + 1)
                hi_part(xnT[:, 0, g0 * N:g1 * N], bank, xnT_hi)

            def qk_part(b, c, bank):
                act.wait_ge(qk_mm, UNITS * b + c + 1)
                act.activation(QK[:, 0, c, :], bank, ACT.Copy).then_inc(qk_hi, 1)

            def exps(b, p, u):
                act.wait_ge(t4_ok, UNITS * b + p + 1)
                act.activation(en[:, p % 4, :], t4[:, p % 4, :], ACT.Exp)
                if not (isinstance(u, int) and u < 2):
                    act.wait_ge(t_done, UNITS * b + p - 1)
                for h in range(2):
                    for q in range(QT):
                        i = h * QT + q
                        last = act.activation(Pr[:, p % 2, h, q, :], S[:, p % 2, h, q * M:(q + 1) * M], ACT.Exp,
                                              bias=nm[:, p % 4, i:i + 1], scale=SCALE,
                                              accum_out=sm[:, p % 4, i:i + 1])
                last.then_inc(exp_done, 1)

            def values(b, i, bank):
                half, kt = i // 2, i % 2
                act.wait_ge(v_mm, VP * b + i + 1)
                act.activation(V[:, kt, half * 512:(half + 1) * 512], bank, ACT.Copy).then_inc(v_sb, 1)

            def probabilities(b, p, both=False):
                act.wait_ge(t_done, UNITS * b + p + 1)
                if both:
                    act.activation(PT[:, p % 2, 0, :], Tb[:, 0, :], ACT.Copy).then_inc(pt_sb, 1)
                act.activation(PT[:, p % 2, 1, :], Tb[:, 1, :], ACT.Copy).then_inc(pt_sb2, 1)

            def o_part(b, p):
                act.wait_ge(pv_done, UNITS * b + p + 1)
                act.activation(O[:, 0, p, :], Ob[:, 0:N], ACT.Copy).then_inc(o_hi, 1)

            wq_part(0)
            ctx_part(ld_ctx0, slice(0, M), ctx0_hi)
            xnT_part(0)
            wk_part(0)
            wq_part(1)
            qk_part(0, 0, lead_banks[0])
            wk_part(1)
            qk_part(0, 1, lead_banks[1])
            wv_part(0)
            ctx_part(ld_ctx1, slice(M, TOK), ctx1_hi)
            qk_part(0, 2, lead_banks[2])
            qk_part(0, 3, lead_banks[3])
            exps(0, 0, 0)
            qk_part(0, 4, lead_banks[4])
            qk_part(0, 5, lead_banks[5])
            wv_part(1)
            exps(0, 1, 1)
            qk_part(0, 6, lead_banks[6])
            xnT_part(1)
            qk_part(0, 7, lead_banks[7])
            xnT_part(2)
            act.wait_ge(wq_lo, 2)
            act.wait_ge(nk_prod, 1)
            values(0, 0, Rb[:, :])
            values(0, 1, Ob[:, :])
            act.wait_ge(ld_wout, 16)
            hi_part(wout_s[:, 0, :, :], wout_raw, wout_hi)
            probabilities(0, 0)
            exps(0, 2, 2)
            probabilities(0, 1)

            def input_transposed(c, bank):
                act.wait_ge(xn2T_mm, c + 1)
                act.activation(xn2T[:, 0, c * CH:(c + 1) * CH], bank[:, :], ACT.Copy).then_inc(xn2T_hi, 1)
                act.wait_ge(wout_lo, 1)
                act.wait_ge(nw_mm, 1)
                act.activation(acc[:, c * CH:(c + 1) * CH], bank[:, :], ACT.Copy).then_inc(acc_ok, 1)

            def body(b, last):
                def next_probabilities(p):
                    if p + 1 < UNITS:
                        probabilities(b, p + 1, last and p + 1 in BOTH)
                    elif not last:
                        probabilities(b + 1, 0)

                for p in range(1, UNITS):
                    with_values = p in (1, 2) or p in (5, 6) and not last
                    o_part(b, p - 1)
                    if p + 2 < UNITS:
                        exps(b, p + 2, None)
                    elif not last:
                        exps(b + 1, p + 2 - UNITS, None)
                    if with_values:
                        if p in (1, 2):
                            values(b, p + 1, Rb[:, :])
                        else:
                            values(b + 1, p - 5, Rb[:, :])
                        next_probabilities(p)
                    if last and p == 7:
                        input_transposed(0, S[:, 0, 1, :])
                    if not last:
                        qk_part(b + 1, p - 1, Rb[:, :])
                    if not with_values:
                        next_probabilities(p)
                o_part(b, UNITS - 1)
                if last:
                    act.activation(spare[:], mhalf[:, 0:1], ACT.Gelu)
                if not last:
                    exps(b + 1, 2, None)
                    probabilities(b + 1, 1)
                act.wait_ge(out_mm, b + 1)
                act.sem_inc(act_past, 1)
                act.activation(yT[:, bass.ds(N * b, N)], (S[:, 1, 0, :] if last else Rb)[:, 0:N], ACT.Copy).then_inc(y_sb, 1)
                if not last:
                    qk_part(b + 1, UNITS - 1, Rb[:, :])

            with act.Fori(0, B - 1) as b:
                body(b, False)
            body(B - 1, True)

            def gelus(k, i):
                for f in range(FC):
                    act.wait_ge(w1_done, 16 * k + 4 * i + f + 1)
                    if not (first_pair(k) and i == 0):
                        act.wait_ge(h_lo, 16 * k + 4 * (i - 1) + f + 1)
                    act.sem_inc(act_past, 1)
                    act.activation(Hf[:, f, :], Hb[f], ACT.Gelu,
                                   bias=b1_sb[:, bass.ds(2 * FC * k + place(k, i)[0] * FC + f, 1)]).then_inc(gelu_done, 1)
                    if f < FC - 1 or peeled(k):
                        if f == 0 and not (first_pair(k) and i == 0):
                            act.wait_ge(w2_done, 4 * k + i)
                        act.wait_ge(gelu_done, 16 * k + 4 * i + f + 1)
                        act.activation(Hs[:, 0, (i % 2) * FC + f, :], Hf[:, f, :],
                                       ACT.Copy).then_inc(h_hi if f < FC - 1 else h_hi3, 1)

            gelus(0, 0)
            input_transposed(1, Rb)
            gelus(0, 1)
            gelus(0, 2)
            gelus(0, 3)
            gelus(1, 0)
            with act.Fori(1, E // 2 - 1) as k:
                for i in range(1, 5):
                    gelus(k, i)
            for i in range(1, 4):
                gelus(E // 2 - 1, i)

        @block.tensor
        def _(pe):
            pe.sem_inc(w2_done, 1)

            def products(dst, left, right):
                steps = [(a[0 + x_], b_[0 + y_]) for a, b_ in zip(left, right) for x_, y_ in SPLIT]
                for n, (a, b_) in enumerate(steps):
                    last = pe.matmul(dst, a, b_, start=n == 0, stop=n == len(steps) - 1)
                return last

            def qk(b, c, bank):
                cols = slice(c * P, (c + 1) * P)
                products(bank[:, 0:N], [[wq_s[:, r, cols] for r in range(2)]],
                         [[xnT[:, r, bass.ds(b * N, N)] for r in range(2)]])
                products(bank[:, N:N + M], [[wk_s[:, r, k, cols] for r in range(2)] for k in range(CK)],
                         [[ctxT[:, r, k, bass.ds(b * M, M)] for r in range(2)] for k in range(CK)]).then_inc(qk_mm, 1)

            def value(b, i, bank):
                half, kt = i // 2, i % 2
                if i == 0:
                    pe.wait_ge(ctxV_ok, 2 * (b + 1))
                products(bank, [[ctxV[:, r, k, kt * P:(kt + 1) * P] for r in range(2)] for k in range(CK)],
                         [[wv_s[:, r, k, half * 512:(half + 1) * 512] for r in range(2)] for k in range(CK)]).then_inc(v_mm, 1)

            def scores(b, p, u):
                pe.wait_ge(qk_lo, UNITS * b + p + 1)
                if not (isinstance(u, int) and u < 2):
                    pe.wait_ge(exp_done, UNITS * b + p - 1)
                for q in range(QT):
                    for n, (i, j) in enumerate(SPLIT):
                        for h in range(2):
                            rows = slice(h * DH, (h + 1) * DH)
                            last = pe.matmul(S[:, p % 2, h, q * M:(q + 1) * M], QK[rows, i, p, q * P:(q + 1) * P],
                                             QK[rows, j, p, N:N + M], start=n == 0, stop=n == len(SPLIT) - 1)
                last.then_inc(s_done, 1)

            def transposes(b, p, u):
                pe.wait_ge(scaled, UNITS * b + p + 1)
                if not (isinstance(u, int) and u < 1):
                    pe.wait_ge(pt_sb, UNITS * b + p)
                    pe.wait_ge(pt_sb2, UNITS * b + p)
                for h in range(2):
                    for q in range(QT):
                        for k in range(KT):
                            last = pe.transpose(Tb[:, h, k * N + q * P:k * N + (q + 1) * P],
                                                Pr[:, p % 2, h, q, k * P:(k + 1) * P], ident[:, :])
                last.then_inc(t_done, 1)

            def attend(b, p):
                pe.wait_ge(pt_sb, UNITS * b + p + 1)
                pe.wait_ge(pt_sb2, UNITS * b + p + 1)
                pe.wait_ge(v_sb, VP * b + (2 if p < UNITS // 2 else 4))
                pe.wait_ge(o_lo, UNITS * b + p + 1)
                for k in range(KT):
                    for h in range(2):
                        head = 2 * p + h
                        last = pe.matmul(Ob[h * DH:(h + 1) * DH, 0:N], V[:, k, head * DH:(head + 1) * DH],
                                         PT[:, p % 2, h, k * N:(k + 1) * N], start=k == 0, stop=k == KT - 1)
                last.then_inc(pv_done, 1)

            def x_transposed(i):
                (g0, g1), bank = XPARTS[i]
                for t in range(QT * g0, QT * g1):
                    pe.wait_ge(xn_ok, t + 1)
                    last = pe.transpose(bank[:, (t - QT * g0) * P:(t - QT * g0 + 1) * P], xn[:, t, :], ident[:, :])
                last.then_inc(xnT_mm, 1)

            def null_keys(ts):
                for t in ts:
                    last = products(Rb[:, t * HEADS:(t + 1) * HEADS],
                                    [[xnT[:, r, t * P:(t + 1) * P] for r in range(2)]], [[NK_s[:, r, :] for r in range(2)]])
                last.then_inc(ns_mm, 1)

            def keep_busy(n):
                for _ in range(n):
                    pe.matmul(Rb[:, 0:P], ident[:, :], ident[:, :], start=True, stop=True)

            pe.wait_ge(ident_ok, 2)
            keep_busy(10)
            x_transposed(0)
            keep_busy(6)
            pe.wait_ge(wq_lo, 1)
            pe.wait_ge(xnT_lo, 1)
            pe.wait_ge(ctx0_lo, CK)
            pe.wait_ge(wk_lo, 1)
            for c in range(2):
                qk(0, c, lead_banks[c])
            scores(0, 0, 0)
            pe.wait_ge(nk_lo, 1)
            null_keys(range(QT))
            pe.wait_ge(wq_lo, 2)
            pe.wait_ge(wk_lo, 2)
            qk(0, 2, lead_banks[2])
            qk(0, 3, lead_banks[3])
            scores(0, 1, 1)
            qk(0, 4, lead_banks[4])
            pe.wait_ge(qk_lo, 3)
            qk(0, 5, lead_banks[5])
            pe.wait_ge(ns_ok, 1)
            pe.wait_ge(nvb_ok, 2)
            pe.wait_ge(ld_wout, 16)
            for c in range(PAIRS):
                last_mm = pe.matmul(Rb[0:HEADS, 0:DIM], NVB[:, c, :], wout_raw[:, c, :], start=c == 0, stop=c == PAIRS - 1)
            last_mm.then_inc(nw_mm, 1)
            pe.wait_ge(qk_lo, 4)
            qk(0, 6, lead_banks[6])
            pe.wait_ge(nw_sb, 1)
            x_transposed(1)
            pe.wait_ge(qk_lo, 5)
            qk(0, 7, lead_banks[7])
            pe.wait_ge(qk_lo, 6)
            x_transposed(2)
            scores(0, 2, 2)
            pe.wait_ge(wv_lo, 1)
            pe.wait_ge(xnT_lo, 2)
            value(0, 0, Rb[:, :])
            pe.wait_ge(xnT_lo, 3)
            value(0, 1, Ob[:, :])
            pe.wait_ge(qk_lo, UNITS)
            transposes(0, 0, 0)
            pe.wait_ge(v_sb, 1)
            null_keys(range(QT, 4))
            scores(0, 3, None)
            null_keys(range(4, 6))
            transposes(0, 1, None)
            null_keys(range(6, TILES))
            attend(0, 0)
            pe.wait_ge(wv_lo, 2)

            def project(b, bank):
                pe.wait_ge(o_lo, UNITS * (b + 1) + 1)
                pe.wait_ge(wout_lo, 1)
                products(bank[:, 0:N], [[wout_s[:, r, c, :] for r in range(2)] for c in range(PAIRS)],
                         [[O[:, r, c, :] for r in range(2)] for c in range(PAIRS)]).then_inc(out_mm, 1)

            def null_transposed(g, bank):
                ts = GROUPS[g]
                pe.wait_ge(pn_ok, UNITS * (ts[-1] + 1) // QT)
                for t in ts:
                    last = pe.transpose(bank[0:HEADS, t % CT * P:(t % CT + 1) * P], pn[:, t, :], ident[:, :])
                last.then_inc(pnT_mm, 1)

            def outputs(g):
                pe.wait_ge(pnT_sb, g + 1)
                if g:
                    pe.wait_ge(x1_ok, g)
                for t in GROUPS[g]:
                    if t % QT == 0:
                        pe.wait_ge(y_sb, t // QT + 1)
                    dst = Rb[:, t % CT * DIM:(t % CT + 1) * DIM]
                    pe.matmul(dst, yT[:, t * P:(t + 1) * P], ident[:, :], start=True, stop=False)
                    last = pe.matmul(dst, pnT[:, t % CT * P:(t % CT + 1) * P], NW[:, :], start=False, stop=True)
                last.then_inc(y_mm, 1)

            def input_transposed(c, bank):
                pe.wait_ge(xn2_ok, (1, len(GROUPS))[c])
                for t in range(CT):
                    last = pe.transpose(bank[:, t * P:(t + 1) * P], xn2[:, c * CT + t, :], ident[:, :])
                last.then_inc(xn2T_mm, 1)

            def logits(c):
                if c == 0:
                    pe.wait_ge(rw_lo, 1)
                    pe.wait_ge(o_lo, UNITS * B + 1)
                pe.wait_ge(xn2T_lo, c + 1)
                for t in range(CT):
                    tok = slice((c * CT + t) * P, (c * CT + t + 1) * P)
                    last = products(Ob[:, t * E:(t + 1) * E], [[xn2T[:, r, tok] for r in range(2)]],
                                    [[rw_s[:, r, :] for r in range(2)]])
                last.then_inc(lg_mm, 1)

            def gates_transposed(c):
                pe.wait_ge(cw_ok, c + 1)
                for t in range(CT):
                    last = pe.transpose(Ob[0:E, t * P:(t + 1) * P], cw[:, t, :], ident[:, :])
                last.then_inc(cwT_mm, 1)

            def body(b, last):
                def next_transposes(p):
                    if p + 1 < UNITS:
                        transposes(b, p + 1, None)
                    elif not last:
                        transposes(b + 1, 0, None)

                for p in range(1, UNITS):
                    with_values = p in (1, 2) or p in (5, 6) and not last
                    if last and p == 7:
                        input_transposed(0, S[:, 0, 1, :])
                    if p + 3 < UNITS:
                        scores(b, p + 3, None)
                    elif not last:
                        scores(b + 1, p + 3 - UNITS, None)
                    if with_values:
                        if last and p == 2:
                            pe.wait_ge(pnT_sb, 1)
                        else:
                            pe.wait_ge(qk_lo, UNITS * (b + 1) + p - 1)
                        if p == 1:
                            pe.wait_ge(ctx1_lo, CK)
                            pe.wait_ge(ns_ok, 2)
                        if p in (1, 2):
                            value(b, p + 1, Rb[:, :])
                        else:
                            value(b + 1, p - 5, Rb[:, :])
                        next_transposes(p)
                        pe.wait_ge(v_sb, VP * b + (p + 2 if p in (1, 2) else p))
                    elif not last:
                        pe.wait_ge(qk_lo, UNITS * (b + 1) + p - 1)
                    if not last:
                        qk(b + 1, p - 1, Rb)
                    elif p == 1:
                        null_transposed(0, Rb)
                    elif p == 2:
                        outputs(0)
                    if not with_values:
                        next_transposes(p)
                    attend(b, p)
                    if last and p in (5, 7):
                        null_transposed((p - 3) // 2, S[:, 0, 0, :])
                    if last and p == 6:
                        outputs(1)
                if not last:
                    scores(b + 1, 3, None)
                    transposes(b + 1, 1, None)
                    pe.wait_ge(qk_lo, UNITS * (b + 2) - 1)
                project(b, S[:, 1, 0, :] if last else Rb)
                if not last:
                    attend(b + 1, 0)
                    pe.wait_ge(y_sb, b + 1)
                    qk(b + 1, UNITS - 1, Rb)

            with pe.Fori(0, B - 1) as b:
                body(b, False)
            body(B - 1, True)

            def up(k, i):
                e, c = place(k, i)
                s = e % 2
                if c == 0:
                    pe.wait_ge(wsplit, 4 * (2 * k + e) + 2)
                for f in range(FC):
                    if not (first_pair(k) and i == 0):
                        pe.wait_ge(gelu_done, 16 * k + 4 * (i - 1) + f + 1)
                    products(Hb[f], [[Ws[:, r, s, f * P:(f + 1) * P] for r in range(2)]],
                             [[xn2T[:, r, c * CH:(c + 1) * CH] for r in range(2)]]).then_inc(w1_done, 1)

            def down(k, i):
                e, c = place(k, i)
                s = e % 2
                if c == 0:
                    pe.wait_ge(wsplit, 4 * (2 * k + e) + 4)
                pe.wait_ge(y_done, 4 * k + i + 1)
                for f in range(FC):
                    pe.wait_ge(h_lo, 16 * k + 4 * i + f + 1)
                    for n, (x_, y_) in enumerate(SPLIT):
                        last = pe.matmul(Yb[i % 2], Ws[:, x_, s, FF + f * P:FF + (f + 1) * P], Hs[:, y_, (i % 2) * FC + f, :],
                                         start=f == 0 and n == 0, stop=f == FC - 1 and n == len(SPLIT) - 1)
                last.then_inc(w2_done, 1)

            logits(0)
            outputs(2)
            up(0, 0)
            gates_transposed(0)
            up(0, 1)
            input_transposed(1, Rb)
            down(0, 0)
            pe.wait_ge(cwT_ok, 1)
            logits(1)
            up(0, 2)
            down(0, 1)
            down(0, 2)
            gates_transposed(1)
            up(0, 3)
            up(1, 0)
            down(0, 3)
            with pe.Fori(1, E // 2 - 1) as k:
                for i in range(4):
                    up(k, i + 1)
                    down(k, i)

            def sums_transposed(n):
                ts, bank = ENDS[n]
                pe.wait_ge(y_done, 2 * E + 1 + n)
                for t in ts:
                    last = pe.transpose(bank[:, (t - ts[0]) * P:(t - ts[0] + 1) * P], acc[:, t * P:(t + 1) * P], ident[:, :])
                last.then_inc(accT_mm, 1)

            def last_down(n):
                cols = slice(n * CH // 2, (n + 1) * CH // 2)
                s = (E - 1) % 2
                if n == 0:
                    pe.wait_ge(wsplit, 4 * E)
                pe.wait_ge(y_done, 2 * E + n)
                steps = [(f, x_, y_) for f in range(FC) for x_, y_ in SPLIT]
                for i, (f, x_, y_) in enumerate(steps):
                    if n == 0 and i % len(SPLIT) == 0:
                        pe.wait_ge(h_lo, FC * (2 * E - 1) + f + 1)
                    last = pe.matmul(Yb[1 - n][:, 0:CH // 2], Ws[:, x_, s, FF + f * P:FF + (f + 1) * P],
                                     Hs[:, y_, FC + f, cols], start=i == 0, stop=i == len(steps) - 1)
                last.then_inc(w2_done, 1)

            for i in range(3):
                up(E // 2 - 1, i + 1)
                down(E // 2 - 1, i)
            last_down(0)
            sums_transposed(0)
            last_down(1)
            sums_transposed(1)
            sums_transposed(2)

        @block.vector
        def _(dve):
            links = [0]

            def link(ins):
                links[0] += 1
                ins.then_inc(dve_link, 1)
                dve.wait_ge(dve_link, links[0])

            dve.sem_inc(o_lo, 1)
            dve.sem_inc(y_done, 2)

            def lo_part(dst, full, hi):
                return dve.tensor_tensor(dst, full, hi.bitcast(F32), ALU.subtract)

            def statistics(src, ts, eps):
                for t in ts:
                    last = dve.bn_stats(st[:, t, :], src[:, t - ts[0], :])
                link(last)
                for t in ts:
                    last = dve.bn_aggr(mv[:, t, :], st[:, t, :])
                link(last)
                dve.tensor_scalar(ve[:, ts[0]:ts[-1] + 1], mv[:, ts[0]:ts[-1] + 1, 1], eps, None, ALU.add).then_inc(var_ok, 1)

            def normalize(dst, src, ts, n):
                dve.wait_ge(rstd_ok, n)
                for t in ts:
                    last = dve.tensor_scalar(dst[:, t - ts[0], :], src[:, t - ts[0], :], mv[:, t, 0:1], rstd[:, t:t + 1],
                                             ALU.subtract, ALU.mult)
                return last

            def normalized(ts, n):
                dve.wait_ge(rstd_ok, n)
                for t in ts:
                    dve.tensor_scalar(xn[:, t, :], x_sb[:, t, :], mv[:, t, 0:1], rstd[:, t:t + 1],
                                      ALU.subtract, ALU.mult).then_inc(xn_ok, 1)

            def xnT_part(i):
                (g0, g1), bank = XPARTS[i]
                cols = slice(g0 * N, g1 * N)
                dve.wait_ge(xnT_hi, i + 1)
                lo_part(xnT[:, 1, cols], bank, xnT[:, 0, cols]).then_inc(xnT_lo, 1)

            def wq_part(h):
                dve.wait_ge(wq_hi, h + 1)
                lo_part(wq_s[:, 1, PART[h]], wq_raw[:, PART[h]], wq_s[:, 0, PART[h]]).then_inc(wq_lo, 1)

            def wk_part(h):
                dve.wait_ge(wk_hi, h + 1)
                lo_part(wk_s[:, 1, :, PART[h]], wk_raw[:, :, PART[h]], wk_s[:, 0, :, PART[h]]).then_inc(wk_lo, 1)

            def null_key():
                dve.wait_ge(nk_prod, 1)
                link(dve.tensor_reduce(NKf[:], y_att[:, :, :].rearrange("p t n -> p (t n)").rearrange("p (h d) -> p h d", d=DH),
                                       AX.X, ALU.add))
                link(dve.tensor_copy(NK_s[:, 0, :], NKf[:]))
                lo_part(NK_s[:, 1, :], NKf[:], NK_s[:, 0, :]).then_inc(nk_lo, 1)

            def null_keys(ts):
                dve.wait_ge(ns_mm, ts[-1] // QT + 1)
                dve.tensor_scalar(nsn[:, ts[0]:ts[-1] + 1, :].rearrange("p t h -> p (t h)"),
                                  Rb[:, ts[0] * HEADS:(ts[-1] + 1) * HEADS], -SCALE, None, ALU.mult).then_inc(ns_ok, 1)

            dve.wait_ge(ld_x0, 16)
            statistics(x_sb[:, 0:QT, :], list(range(QT)), EPS_PRE)
            wq_part(0)
            normalized(range(QT), 1)
            for k in range(CK):
                dve.wait_ge(ctx0_hi, k + 1)
                lo_part(ctxT[:, 1, k, 0:M], ctx_raw[k][:, 0:M], ctxT[:, 0, k, 0:M]).then_inc(ctx0_lo, 1)
            xnT_part(0)
            wk_part(0)
            wq_part(1)

            def qk_part(b, c, bank):
                dve.wait_ge(qk_hi, UNITS * b + c + 1)
                lo_part(QK[:, 1, c, :], bank, QK[:, 0, c, :]).then_inc(qk_lo, 1)

            def null_scores(src, b, p):
                return src[:, bass.ds(QT * b, QT), 2 * p:2 * p + 2].rearrange("p t h -> p h t")

            def by_head(small, p):
                return small[:, p % 4, :].rearrange("p (h t) -> p h t", h=2)

            def maxima(new, old):
                if new:
                    b, p = new
                    dve.wait_ge(s_done, UNITS * b + p + 1)
                    dve.tensor_reduce(mx[:, p % 4, :], S[:, p % 2, :, :].rearrange("p h (t m) -> p (h t) m", m=M), AX.X, ALU.max,
                                      negate=True).then_inc(mx_ok, 1)
                if old:
                    c, r = old
                    dve.wait_ge(exp_done, UNITS * c + r + 1)
                    dve.tensor_tensor(den[:, r % 4, :], sm[:, r % 4, :], en[:, r % 4, :], ALU.add).then_inc(den_ok, 1)
                if new:
                    dve.wait_ge(mx_ok, UNITS * b + p + 1)
                    dve.scalar_tensor_tensor(by_head(nm, p), by_head(mx, p), SCALE, null_scores(nsn, b, p),
                                             ALU.mult, ALU.min).then_inc(nm_ok, 1)
                if old:
                    dve.wait_ge(den_ok, UNITS * c + r + 1)
                    dve.reciprocal(rden[:, r % 4, :], den[:, r % 4, :]).then_inc(rden_ok, 1)
                if new:
                    dve.wait_ge(nm_ok, UNITS * b + p + 1)
                    dve.tensor_tensor(by_head(t4, p), by_head(nm, p), null_scores(nsn, b, p), ALU.subtract).then_inc(t4_ok, 1)
                if old:
                    dve.wait_ge(rden_ok, UNITS * c + r + 1)
                    dve.tensor_tensor(null_scores(pn, c, r), by_head(en, r), by_head(rden, r), ALU.mult).then_inc(pn_ok, 1)

            def probabilities(b, p):
                dve.wait_ge(t_done, UNITS * b + p + 1)
                dve.tensor_copy(PT[:, p % 2, 0, :], Tb[:, 0, :]).then_inc(pt_sb, 1)

            def o_part(b, p):
                dve.wait_ge(o_hi, UNITS * b + p + 1)
                lo_part(O[:, 1, p, :], Ob[:, 0:N], O[:, 0, p, :]).then_inc(o_lo, 1)

            qk_part(0, 0, lead_banks[0])
            null_key()
            wk_part(1)
            dve.wait_ge(const_ok, 4)
            for h in range(2):
                rows = slice(h * DH, (h + 1) * DH)
                flat = NVB[rows, :, :].rearrange("p c h -> p (c h)")
                dve.tensor_copy(flat[:, h:(PAIRS - 1) * (HEADS + 2) + h + 1:HEADS + 2],
                                nv_col[rows, 0:1].to_broadcast([DH, PAIRS])).then_inc(nvb_ok, 1)

            null_keys(range(QT))
            qk_part(0, 1, lead_banks[1])
            maxima((0, 0), None)
            dve.wait_ge(ld_x, 16)
            statistics(x_sb[:, QT:TILES, :], list(range(QT, TILES)), EPS_PRE)
            qk_part(0, 2, lead_banks[2])
            qk_part(0, 3, lead_banks[3])
            normalized(range(QT, TILES), 2)
            maxima((0, 1), (0, 0))
            qk_part(0, 4, lead_banks[4])
            qk_part(0, 5, lead_banks[5])
            dve.wait_ge(nw_mm, 1)
            dve.tensor_copy(NW[:, :], Rb[0:HEADS, 0:DIM]).then_inc(nw_sb, 1)
            qk_part(0, 6, lead_banks[6])
            xnT_part(1)
            qk_part(0, 7, lead_banks[7])
            xnT_part(2)
            maxima((0, 2), (0, 1))
            probabilities(0, 0)
            maxima((0, 3), (0, 2))
            probabilities(0, 1)
            null_keys(range(QT, TILES))
            def scaled_norm(dst, src, ts, w):
                for n, t in enumerate(ts):
                    last = dve.scalar_tensor_tensor(dst[:, n, :], src[:, n, :], mv[:, t, 0:1], w, ALU.subtract, ALU.mult)
                link(last)

            def residual(dst, plus, ts, n):
                dve.wait_ge(rstd_ok, n)
                for i, t in enumerate(ts):
                    last = dve.scalar_tensor_tensor(dst[:, i, :], dst[:, i, :], rstd[:, t:t + 1], plus[:, i, :],
                                                    ALU.mult, ALU.add)
                return last

            link(dve.tensor_copy(rw_s[:, 0, :], rw_f))
            lo_part(rw_s[:, 1, :], rw_f, rw_s[:, 0, :]).then_inc(rw_lo, 1)

            def null_transposed(g, bank):
                cols = slice(GROUPS[g][0] % CT * P, (GROUPS[g][-1] % CT + 1) * P)
                dve.wait_ge(pnT_mm, g + 1)
                dve.tensor_copy(pnT[:, cols], bank[0:HEADS, cols]).then_inc(pnT_sb, 1)

            def output(g):
                ts = GROUPS[g]
                return Rb[:, ts[0] % CT * DIM:(ts[-1] % CT + 1) * DIM].rearrange("p (t n) -> p t n", t=len(ts))

            def output_statistics(g):
                dve.wait_ge(y_mm, g + 1)
                statistics(output(g), GROUPS[g], EPS_ATT)

            def attended(g):
                ts = GROUPS[g]
                t = slice(ts[0], ts[-1] + 1)
                scaled_norm(x1[:, t, :], output(g), ts, l1w)
                dve.wait_ge(xb_ok, 1)
                residual(x1[:, t, :], x_sb[:, t, :], ts, NORMS + 1 + 2 * g).then_inc(x1_ok, 1)

            def input_statistics(g):
                ts = GROUPS[g]
                dve.wait_ge(x1_ok, g + 1)
                statistics(x1[:, ts[0]:ts[-1] + 1, :], ts, EPS_PRE)

            def experts_input(g):
                ts = GROUPS[g]
                t = slice(ts[0], ts[-1] + 1)
                normalize(xn2[:, t, :], x1[:, t, :], ts, NORMS + 2 + 2 * g).then_inc(xn2_ok, 1)

            def input_transposed(c, bank):
                tok = slice(c * CH, (c + 1) * CH)
                dve.wait_ge(acc_ok, c + 1)
                lo_part(xn2T[:, 1, tok], bank[:, :], xn2T[:, 0, tok]).then_inc(xn2T_lo, 1)

            def largest(c):
                dve.wait_ge(lg_mm, c + 1)
                dve.tensor_tensor(lg[:], Ob[:, 0:CT * E].rearrange("p (t e) -> p t e", t=CT),
                                  rb_b[:, None, :].to_broadcast([P, CT, E]), ALU.add).then_inc(lg_ok, 1)
                dve.wait_ge(lg_ok, c + 1)
                for i in range(CT):
                    last = dve.max(top[:, i, :], lg[:, i, :])
                link(last)
                dve.tensor_tensor(gd[:], top[:, :, 1], top[:, :, 0], ALU.subtract).then_inc(gap_ok, 1)
                for i in range(CT):
                    last = dve.max_index(topi[:, i, :], top[:, i, :], lg[:, i, :])
                link(last)
                link(dve.tensor_copy(topf[:], topi[:]))
                for n, chosen in enumerate((ca, cb)):
                    last = dve.tensor_tensor(chosen[:], iota8[:, None, :].to_broadcast([P, CT, E]),
                                             topf[:, :, n:n + 1].to_broadcast([P, CT, E]), ALU.is_equal)
                link(last)

            def gates(c):
                dve.wait_ge(ge_ok, c + 1)
                link(dve.tensor_scalar(g1[:], ge[:], 1.0, None, ALU.add))
                link(dve.reciprocal(gw0[:], g1[:]))
                link(dve.tensor_tensor(gw1[:], ge[:], gw0[:], ALU.mult))
                dve.tensor_tensor(ca[:], ca[:], gw0[:, :, None].to_broadcast([P, CT, E]), ALU.mult)
                link(dve.tensor_tensor(cb[:], cb[:], gw1[:, :, None].to_broadcast([P, CT, E]), ALU.mult))
                dve.tensor_tensor(cw[:], ca[:], cb[:], ALU.add).then_inc(cw_ok, 1)

            def gates_transposed(c):
                dve.wait_ge(cwT_mm, c + 1)
                if c:
                    dve.wait_ge(cw_st, 16 * c)
                dve.tensor_copy(cwT[:, :], Ob[0:E, :]).then_inc(cwT_ok, 1)

            def body(b, last):
                def unit(p):
                    return (b, p) if p < UNITS else None if last else (b + 1, p - UNITS)

                for p in range(1, UNITS):
                    o_part(b, p - 1)
                    maxima(unit(p + 3), unit(p + 2))
                    with_values = p in (1, 2) or p in (5, 6) and not last
                    copies = unit(p + 1) and not (last and p + 1 in BOTH)
                    if with_values and copies:
                        probabilities(*unit(p + 1))
                    if not last:
                        qk_part(b + 1, p - 1, Rb[:, :])
                    if not with_values and copies:
                        probabilities(*unit(p + 1))
                    if last:
                        if p == 1:
                            null_transposed(0, Rb)
                        elif p == 3:
                            output_statistics(0)
                        elif p == 4:
                            attended(0)
                        elif p == 5:
                            input_statistics(0)
                            null_transposed(1, S[:, 0, 0, :])
                        elif p == 6:
                            experts_input(0)
                        elif p == 7:
                            input_transposed(0, S[:, 0, 1, :])
                o_part(b, UNITS - 1)
                if not last:
                    maxima((b + 1, 3), (b + 1, 2))
                    probabilities(b + 1, 1)
                    qk_part(b + 1, UNITS - 1, Rb[:, :])

            with dve.Fori(0, B - 1) as b:
                body(b, False)
            body(B - 1, True)

            def hidden(k, i, fs=range(FC)):
                for f in fs:
                    slot = (i % 2) * FC + f
                    if f < FC - 1:
                        dve.wait_ge(h_hi, 12 * k + 3 * i + f + 1)
                    else:
                        if not peeled(k):
                            dve.wait_ge(gelu_done, 16 * k + 4 * i + FC)
                            dve.tensor_copy(Hs[:, 0, slot, :], Hf[:, f, :]).then_inc(h_hi3, 1)
                        dve.wait_ge(h_hi3, 4 * k + i + 1)
                    lo_part(Hs[:, 1, slot, :], Hf[:, f, :], Hs[:, 0, slot, :]).then_inc(h_lo, 1)

            def gather(k, i):
                e, c = place(k, i)
                dve.wait_ge(cwB_ok[i % 2], 32 * k + 16 * (i // 2 + 1))
                dve.wait_ge(w2_done, 4 * k + i + 2)
                dve.wait_ge(y_done, 4 * k + i + 2)
                dve.scalar_tensor_tensor(tmp[:], Yb[i % 2], b2_sb[:, bass.ds(2 * k + e, 1)], cwB[:, i % 2, :],
                                         ALU.add, ALU.mult).then_inc(y_part, 1)
                if first_pair(k):
                    dve.wait_ge(acc_ok, c + 1)
                dve.wait_ge(y_part, 4 * k + i + 1)
                part = acc[:, c * CH:(c + 1) * CH]
                dve.tensor_tensor(part, part, tmp[:], ALU.add).then_inc(y_done, 1)

            output_statistics(1)
            null_transposed(2, S[:, 0, 0, :])
            attended(1)
            input_statistics(1)
            largest(0)
            experts_input(1)
            output_statistics(2)
            gates(0)
            attended(2)
            input_statistics(2)
            hidden(0, 0, (0,))
            experts_input(2)
            gates_transposed(0)
            hidden(0, 0, (1, 2, 3))
            input_transposed(1, Rb)
            hidden(0, 1)
            gather(0, 0)
            largest(1)
            hidden(0, 2)
            gates(1)
            gather(0, 1)
            gates_transposed(1)
            hidden(0, 3)
            hidden(1, 0, (0, 1))
            gather(0, 2)
            hidden(1, 0, (2, 3))
            gather(0, 3)
            with dve.Fori(1, E // 2 - 1) as k:
                for i in range(4):
                    hidden(k, i + 1)
                    gather(k, i)
            for i in range(3):
                hidden(E // 2 - 1, i + 1)
                gather(E // 2 - 1, i)

            def last_gather(n):
                cols = slice(n * CH // 2, (n + 1) * CH // 2)
                dve.wait_ge(w2_done, 2 * E + 1 + n)
                dve.wait_ge(y_done, 2 * E + 1 + n)
                dve.wait_ge(cwB_ok[1], 16 * E)
                dve.scalar_tensor_tensor(tmp[:, cols], Yb[1 - n][:, 0:CH // 2], b2_sb[:, E - 1:E], cwB[:, 1, cols],
                                         ALU.add, ALU.mult).then_inc(y_part, 1)
                dve.wait_ge(y_part, 2 * E + n)
                part = acc[:, CH + n * CH // 2:CH + (n + 1) * CH // 2]
                dve.tensor_tensor(part, part, tmp[:, cols], ALU.add).then_inc(y_done, 1)

            def sums(n):
                ts, bank = ENDS[n]
                return bank[:, 0:len(ts) * DIM].rearrange("p (t n) -> p t n", t=len(ts))

            def sum_statistics(n):
                dve.wait_ge(accT_mm, n + 1)
                statistics(sums(n), ENDS[n][0], EPS_MOE)

            def scaled_sums(n):
                ts = ENDS[n][0]
                scaled_norm(y_att[:, ts[0]:ts[-1] + 1, :], sums(n), ts, l2w)

            def result(n):
                ts = ENDS[n][0]
                t = slice(ts[0], ts[-1] + 1)
                dve.wait_ge(xb_ok, 2)
                residual(y_att[:, t, :], x_sb[:, t, :], ts, NORMS + 1 + 2 * len(GROUPS) + n).then_inc(res_ok, 1)

            last_gather(0)
            sum_statistics(0)
            last_gather(1)
            sum_statistics(1)
            scaled_sums(0)
            sum_statistics(2)
            result(0)
            scaled_sums(1)
            result(1)
            scaled_sums(2)
            result(2)


def kernel(**inputs):
    import numpy as np
    import concourse.bacc as bacc
    from concourse.bass_utils import run_bass_kernel_spmd

    a = {k: np.asarray(v) for k, v in inputs.items()}
    wkv = a["L0_xattn_Wkv"]

    def tiles(w):
        return w.reshape(-1, P, w.shape[1]).transpose(1, 0, 2)

    w1, w2 = a["L0_ffn_w1"], a["L0_ffn_w2"]
    laid = {
        "x": a["x"].reshape(TILES, P, DIM).transpose(1, 0, 2),
        "ctx_t": tiles(a["ctx_2048"].reshape(B * M, CTX).T),
        "wq": a["L0_xattn_Wq"],
        "wk": tiles(wkv[:, :INNER]),
        "wv": tiles(wkv[:, INNER:]),
        "wout": tiles(a["L0_xattn_Wout"]),
        "rows": np.concatenate([a["L0_xattn_ln_scale"], a["L0_xattn_ln_bias"], a["L0_ffn_ln_w"], a["L0_ffn_ln_b"],
                                a["L0_ffn_router_b"], a["L0_xattn_null_kv"][0]])[None],
        "columns": np.concatenate([a["L0_ffn_b1"].reshape(E * FC, P).T, a["L0_ffn_b2"].T, a["L0_ffn_router_w"].T,
                                   np.concatenate([a["L0_xattn_null_kv"][1]] * 2)[:, None]], axis=1),
        "w1_t": w1.transpose(0, 2, 1),
        "w2_t": w2.reshape(E, DIM, FC, P).transpose(0, 3, 2, 1).reshape(E, P, FF),
    }
    laid = {k: np.ascontiguousarray(v) for k, v in laid.items()}
    nc = bacc.Bacc("TRN2", target_bir_lowering=False, num_devices=1)
    args = {k: nc.dram_tensor(f"in_{k}", v.shape, mybir.dt.from_np(v.dtype), kind="ExternalInput").ap() for k, v in laid.items()}
    out = nc.dram_tensor("out_0", (P, TILES, DIM), F32, kind="ExternalOutput").ap()
    build(nc, *args.values(), out)
    r = run_bass_kernel_spmd(nc, [{f"in_{k}": v for k, v in laid.items()}], core_ids=[0])
    got = r.results[0]["out_0"]
    return got.transpose(1, 0, 2).reshape(B, N, DIM)
```
